# Optimizing a Trainium2 kernel written in Bass

```python
import numpy as np
import jax
import jax.numpy as jnp

def _softmax(x, axis=-1):
    return jax.nn.softmax(x, axis=axis)

def _gelu(x):
    return jax.nn.gelu(x, approximate=True)

def _silu(x):
    return jax.nn.silu(x)

def _sigmoid(x):
    return jax.nn.sigmoid(x)

def _layernorm(x, axis=-1, eps=1e-05):
    m = jnp.mean(x, axis=axis, keepdims=True)
    v = jnp.var(x, axis=axis, keepdims=True)
    return (x - m) / jnp.sqrt(v + eps)

def _scatter_add(tgt, idx, src, axis=0):
    return tgt.at[idx].add(src)

def _segment_sum(src, seg, n):
    return jax.ops.segment_sum(src, seg, n)
kernel_name = 'mk_macaron_d1_jaxref_r8_e6e42c'

def setup_inputs(seed: int=0):
    np.random.seed(seed)
    _w = jnp.asarray

    def _L0_attn_setup():
        import jax, jax.numpy as jnp
        import numpy as np
        H = 128
        D_IN = 256
        N = 16
        K = 4
        R = 128
        EPS = 1e-06

        def _rmsnorm(x, w):
            var = jnp.mean(jnp.square(x), axis=-1, keepdims=True)
            return x * jax.lax.rsqrt(var + EPS) * w

        def _selective_scan(x, dt, Bm, Cm, A_log, D_param):
            A = -jnp.exp(A_log)

            def step(h, inp):
                dt_t, B_t, C_t, x_t = inp
                dA = jnp.exp(dt_t[..., None] * A[None])
                h = dA * h + (dt_t * x_t)[..., None] * B_t[:, None, :]
                y = jnp.einsum('bdn,bn->bd', h, C_t)
                return (h, y)
            B_, L_, d = x.shape
            h0 = jnp.zeros((B_, d, A.shape[1]), jnp.float32)
            xs = (dt.swapaxes(0, 1), Bm.swapaxes(0, 1), Cm.swapaxes(0, 1), x.swapaxes(0, 1))
            _, ys = jax.lax.scan(step, h0, xs)
            return ys.swapaxes(0, 1) + D_param * x
        key = jax.random.key(seed)
        ks = jax.random.split(key, 12)
        B, L = (2, 256)
        s = lambda *sh: 1.0 / np.sqrt(sh[-1])
        inp = {'x': jax.random.normal(ks[0], (B, L, H), jnp.float32), 'norm_w': jnp.ones((H,), jnp.float32), 'in_proj_w': jax.random.normal(ks[1], (2 * D_IN, H), jnp.float32) * s(H), 'conv_w': jax.random.normal(ks[2], (D_IN, 1, K), jnp.float32) * s(K), 'conv_b': jnp.zeros((D_IN,), jnp.float32), 'x_proj_w': jax.random.normal(ks[3], (R + 2 * N, D_IN), jnp.float32) * s(D_IN), 'dt_proj_w': jax.random.normal(ks[4], (D_IN, R), jnp.float32) * D_IN ** (-0.5), 'dt_proj_b': jax.random.uniform(ks[5], (D_IN,), jnp.float32, 0.001, 0.1), 'A_log': jnp.log(jnp.broadcast_to(jnp.arange(1, N + 1, dtype=jnp.float32), (D_IN, N))), 'D_param': jnp.ones((D_IN,), jnp.float32), 'out_proj_w': jax.random.normal(ks[6], (H, D_IN), jnp.float32) * s(D_IN)}
        return inp
    _L0_attn_in = _L0_attn_setup()

    def _L0_ffn_setup():
        import jax, jax.numpy as jnp
        import numpy as np
        H = 128
        I = 128
        E = 8
        key = jax.random.key(seed)
        ks = jax.random.split(key, 8)
        s = 0.02
        x = jax.random.normal(ks[0], (4, 256, H), dtype=jnp.float32)
        Wg = jax.random.normal(ks[1], (H, E), dtype=jnp.float32) * s
        bg = jnp.zeros((E,), dtype=jnp.float32)
        W1 = jax.random.normal(ks[2], (E, H, I), dtype=jnp.float32) * s
        b1 = jnp.zeros((E, I), dtype=jnp.float32)
        W2 = jax.random.normal(ks[3], (E, I, H), dtype=jnp.float32) * s
        b2 = jnp.zeros((E, H), dtype=jnp.float32)
        return {'x': x, 'Wg': Wg, 'bg': bg, 'W1': W1, 'b1': b1, 'W2': W2, 'b2': b2}
    _L0_ffn_in = _L0_ffn_setup()
    _d = {'L0_attn_x': _L0_attn_in['x'], 'L0_attn_norm_w': _L0_attn_in['norm_w'], 'L0_attn_in_proj_w': _L0_attn_in['in_proj_w'], 'L0_attn_conv_w': _L0_attn_in['conv_w'], 'L0_attn_conv_b': _L0_attn_in['conv_b'], 'L0_attn_x_proj_w': _L0_attn_in['x_proj_w'], 'L0_attn_dt_proj_w': _L0_attn_in['dt_proj_w'], 'L0_attn_dt_proj_b': _L0_attn_in['dt_proj_b'], 'L0_attn_A_log': _L0_attn_in['A_log'], 'L0_attn_D_param': _L0_attn_in['D_param'], 'L0_attn_out_proj_w': _L0_attn_in['out_proj_w'], 'L0_ffn_Wg': _L0_ffn_in['Wg'], 'L0_ffn_bg': _L0_ffn_in['bg'], 'L0_ffn_W1': _L0_ffn_in['W1'], 'L0_ffn_b1': _L0_ffn_in['b1'], 'L0_ffn_W2': _L0_ffn_in['W2'], 'L0_ffn_b2': _L0_ffn_in['b2']}
    _x0 = _d['L0_attn_x']
    _d['L0_attn_x'] = jax.random.normal(jax.random.fold_in(jax.random.key(seed), 1), (32, 256, 128), dtype=_x0.dtype)
    del _x0
    return _d

def reference(L0_attn_x, L0_attn_norm_w, L0_attn_in_proj_w, L0_attn_conv_w, L0_attn_conv_b, L0_attn_x_proj_w, L0_attn_dt_proj_w, L0_attn_dt_proj_b, L0_attn_A_log, L0_attn_D_param, L0_attn_out_proj_w, L0_ffn_Wg, L0_ffn_bg, L0_ffn_W1, L0_ffn_b1, L0_ffn_W2, L0_ffn_b2):

    def _L0_attn_ref(x, norm_w, in_proj_w, conv_w, conv_b, x_proj_w, dt_proj_w, dt_proj_b, A_log, D_param, out_proj_w):
        import jax, jax.numpy as jnp
        import numpy as np
        H = 128
        D_IN = 256
        N = 16
        K = 4
        R = 128
        EPS = 1e-06

        def _rmsnorm(x, w):
            var = jnp.mean(jnp.square(x), axis=-1, keepdims=True)
            return x * jax.lax.rsqrt(var + EPS) * w

        def _selective_scan(x, dt, Bm, Cm, A_log, D_param):
            A = -jnp.exp(A_log)

            def step(h, inp):
                dt_t, B_t, C_t, x_t = inp
                dA = jnp.exp(dt_t[..., None] * A[None])
                h = dA * h + (dt_t * x_t)[..., None] * B_t[:, None, :]
                y = jnp.einsum('bdn,bn->bd', h, C_t)
                return (h, y)
            B_, L_, d = x.shape
            h0 = jnp.zeros((B_, d, A.shape[1]), jnp.float32)
            xs = (dt.swapaxes(0, 1), Bm.swapaxes(0, 1), Cm.swapaxes(0, 1), x.swapaxes(0, 1))
            _, ys = jax.lax.scan(step, h0, xs)
            return ys.swapaxes(0, 1) + D_param * x
        residual = x
        xn = _rmsnorm(x, norm_w)
        xz = xn @ in_proj_w.T
        x_path, z_path = jnp.split(xz, 2, axis=-1)
        xc = x_path.swapaxes(1, 2)
        xc = jax.lax.conv_general_dilated(xc, conv_w, window_strides=(1,), padding=[(K - 1, 0)], feature_group_count=D_IN, dimension_numbers=('NCH', 'OIH', 'NCH'))
        xc = xc + conv_b[None, :, None]
        x_path = jax.nn.silu(xc.swapaxes(1, 2))
        x_dbl = x_path @ x_proj_w.T
        dt_x, Bm, Cm = (x_dbl[..., :R], x_dbl[..., R:R + N], x_dbl[..., R + N:])
        dt = jax.nn.softplus(dt_x @ dt_proj_w.T + dt_proj_b)
        y = _selective_scan(x_path.astype(jnp.float32), dt.astype(jnp.float32), Bm.astype(jnp.float32), Cm.astype(jnp.float32), A_log.astype(jnp.float32), D_param.astype(jnp.float32))
        y = y.astype(x.dtype) * jax.nn.silu(z_path)
        return y @ out_proj_w.T + residual

    def _L0_ffn_ref(x, Wg, bg, W1, b1, W2, b2):
        import jax, jax.numpy as jnp
        import numpy as np
        H = 128
        I = 128
        E = 8
        B, S, Hd = x.shape
        xf = x.reshape(-1, Hd)
        logits = xf @ Wg + bg
        gates = jax.nn.softmax(logits, axis=-1)
        idx = jnp.argmax(gates, axis=-1)
        h = jax.nn.gelu(jnp.einsum('th,ehi->tei', xf, W1) + b1, approximate=False)
        y = jnp.einsum('tei,eih->teh', h, W2) + b2
        out = jnp.take_along_axis(y, idx[:, None, None], axis=1)[:, 0, :]
        return out.reshape(B, S, Hd)
    x = L0_attn_x
    x = x + 0.5 * _L0_ffn_ref(_layernorm(x, axis=-1), L0_ffn_Wg, L0_ffn_bg, L0_ffn_W1, L0_ffn_b1, L0_ffn_W2, L0_ffn_b2)
    x = x + _L0_attn_ref(_layernorm(x, axis=-1), L0_attn_norm_w, L0_attn_in_proj_w, L0_attn_conv_w, L0_attn_conv_b, L0_attn_x_proj_w, L0_attn_dt_proj_w, L0_attn_dt_proj_b, L0_attn_A_log, L0_attn_D_param, L0_attn_out_proj_w)
    x = x + 0.5 * _L0_ffn_ref(_layernorm(x, axis=-1), L0_ffn_Wg, L0_ffn_bg, L0_ffn_W1, L0_ffn_b1, L0_ffn_W2, L0_ffn_b2)
    return x

_drawn_inputs = setup_inputs


def setup_inputs(seed=0):
    import zlib

    import numpy as np

    out = dict(_drawn_inputs(seed))
    spreads = {'L0_attn_norm_w': (1.0, 0.2),
     'L0_attn_conv_b': (0.0, 0.1),
     'L0_attn_D_param': (1.0, 0.2),
     'L0_ffn_bg': (0.0, 0.1),
     'L0_ffn_b1': (0.0, 0.8),
     'L0_ffn_b2': (0.0, 0.1)}
    factors = {'L0_attn_dt_proj_b': 8.0, 'L0_ffn_W1': 2.864}
    for name, (base, spread) in spreads.items():
        noise = np.random.default_rng([zlib.crc32(name.encode()), seed]).standard_normal(out[name].shape)
        drawn = base * np.exp(spread * noise) if base else spread * noise
        out[name] = jnp.asarray(drawn.astype(out[name].dtype))
    for name, factor in factors.items():
        out[name] = (out[name] * factor).astype(out[name].dtype)
    return out
```

```python
from contextlib import ExitStack

import concourse.bass as bass
import numpy as np
from concourse import mybir

F32 = mybir.dt.float32
BF16 = mybir.dt.bfloat16
ALU = mybir.AluOpType
ACT = mybir.ActivationFunctionType
AX_X = mybir.AxisListType.X

P = 128
H = 128
L = 256
NTOK = 32 * L
CH = 2 * L
NB = CH // L
J = CH // P
NCH = NTOK // CH
DI = 256
HF = DI // P
N = 16
SLOTS = N
K = 4
R = 128
E = 8
BIG = 1.0e30
LN_EPS, RMS_EPS = 1e-5, 1e-6

FIRST, LAST = -3, NCH + 1
LOOP0, LOOP1 = 2, NCH - 4

G_SEQ = [("ln_p", 1, 1), ("out", 0, -1), ("x1", 1, 1), ("x0", 0, 1), ("z0", 0, 1), ("z1", 1, 1),
         ("dtx", 0, 1), ("bc", 1, 1), ("y_f1", 0, 2), ("dt0", 0, 1), ("dt1", 1, 1), ("y_f2", 0, -2),
         ("ln_f1", 1, 3), ("ln_f2", 0, -1), ("gate_f1", 1, 3), ("gate_f2", 0, -1),
         ("oh_f1", 1, 3), ("oh_f2", 0, -1)]
G_AT = {name: (bank, off) for name, bank, off in G_SEQ}
UNITS = [0, 2, 1, 2, 2, 2, 2, 1, 1, 2, 1, 0, 0, 0, 0, 0]
UNITS[8] += 2 * E - sum(UNITS)
FRONT = {0: 3, 1: -1}
EXPERT = {0: 2, 1: -2}


def g_uses(i, name):
    bank = G_AT[name][0]
    n = sum(0 <= k + off < NCH for k in range(FIRST, i) for _, b, off in G_SEQ if b == bank)
    for other, b, off in G_SEQ:
        if other == name:
            return n
        n += b == bank and 0 <= i + off < NCH


G_EACH = [sum(b == bank for _, b, _ in G_SEQ) for bank in range(2)]


class Iteration:

    def __init__(self, i0, turn=None):
        self.i0, self.turn = i0, turn

    def value(self, at_i0, each):
        return at_i0 if self.turn is None else at_i0 + 2 * each * self.turn

    def has(self, off):
        return 0 <= self.i0 + off < NCH

    def wait(self, eng, sem, off, each, k):
        n = each * (self.i0 + off) + k
        if n > 0:
            eng.wait_ge(sem, self.value(n, each))

    def wait_full(self, eng, g_full, name):
        bank = G_AT[name][0]
        eng.wait_ge(g_full[bank], self.value(g_uses(self.i0, name) + 1, G_EACH[bank]))

    def wait_read(self, eng, g_free, name):
        bank = G_AT[name][0]
        eng.wait_ge(g_free[bank], self.value(g_uses(self.i0, name) + 1, G_EACH[bank]))

    def wait_free(self, eng, g_free, name):
        bank, n = G_AT[name][0], g_uses(self.i0, name)
        if n > 0:
            eng.wait_ge(g_free[bank], self.value(n, G_EACH[bank]))

    def tiles(self, off, j=0, n=J):
        return bass.ds(self.value(J * (self.i0 + off) + j, J), n)


def schedule(eng, body):
    for i in range(FIRST, LOOP0):
        body(Iteration(i))
    with eng.Fori(0, (LOOP1 - LOOP0) // 2) as turn:
        body(Iteration(LOOP0, turn))
        body(Iteration(LOOP0 + 1, turn))
    for i in range(LOOP0 + (LOOP1 - LOOP0) // 2 * 2, LAST + 1):
        body(Iteration(i))


def slot_units(s):
    at = sum(UNITS[:s])
    return [(u // E, u % E) for u in range(at, at + UNITS[s])]


def macaron_kernel(nc, x, winT, wxT, wdtT, woT, norm_w, conv_w, conv_b, dt_b, a_log, d_param,
                   wg, bg, w1, b1, w2, b2, ident, rank, pick, diag, block, out):
    with ExitStack() as ctx:
        def sb(name, shape, dt=F32):
            return ctx.enter_context(nc.sbuf_tensor(name, shape, dt))

        def psum(name, shape):
            return ctx.enter_context(nc.psum_tensor(name, shape, F32))

        def sem(name):
            return ctx.enter_context(nc.semaphore(name))

        X = sb("X", [P, NCH * J, H])
        Win = sb("Win", [P, 2 * DI])
        Wx = sb("Wx", [P, HF, R])
        Wbc = sb("Wbc", [P, HF, 3 * 2 * N])
        Wdt = sb("Wdt", [P, DI])
        Wo = sb("Wo", [P, HF, H])
        Wn = sb("Wn", [P, 1])
        Wc = sb("Wc", [P, HF, K])
        Bc = sb("Bc", [P, HF])
        Bdt = sb("Bdt", [P, HF])
        A = sb("A", [P, HF, N])
        D = sb("D", [P, HF])
        Wg = sb("Wg", [P, E])
        Bg = sb("Bg", [P, J * E])
        W1 = sb("W1", [P, E, P])
        W2 = sb("W2", [P, E, H])
        b_part = sb("b_part", [3 * E, 2, P], BF16)
        Lm = sb("Lm", [3 * E, E, P], BF16)
        Id = sb("Id", [P, P])
        Idb = sb("Idb", [P, P], BF16)
        Rank = sb("Rank", [P, J * E])
        Pick = sb("Pick", [3 * 2 * N, 2 * N, P], BF16)
        ticket = sb("ticket", [P, 2])
        eps = sb("eps", [P, 2, J])
        half = sb("half", [P, 2 * J])
        stat = sb("stat", [P, 3, J, 6])
        mv = sb("mv", [P, 3, J, 2])
        vt = sb("vt", [P, 3, J])
        rstd = sb("rstd", [P, 3, J])
        rms = sb("rms", [P, 2, J])
        xn = sb("xn", [P, 2, J, H])
        xnT = sb("xnT", [P, 2, CH])
        xrT = sb("xrT", [P, CH])
        lg = sb("lg", [P, 2, J, E])
        eq = sb("eq", [P, 2, J, E])
        mx = sb("mx", [P, 2, 2, J])
        oh = sb("oh", [P, 2, J, 3, E], BF16)
        ohT = sb("ohT", [3 * E, 2, CH], BF16)
        hs = sb("hs", [P, 2, CH])
        yT = sb("yT", [P, CH])
        xp = sb("xp", [P, HF, NB, K - 1 + L])
        xs = sb("xs", [P, 2, HF, NB, L])
        zs = sb("zs", [P, 2, HF, CH])
        T3 = sb("T3", [3 * 2 * N, 2, CH], BF16)
        sp = sb("sp", [P, HF, CH])
        dt = sb("dt", [P, HF, NB, L])
        dtx = sb("dtx", [P, 2, HF, CH])
        dA = sb("dA", [P, N, HF, NB, L])
        hb = sb("hb", [P, 4, HF, CH])
        pair = sb("pair", [P, 2, HF, CH])
        y2 = sb("y2", [P, HF, CH])
        set_buf = [hb[0:3 * E, k].rearrange("p h t -> p (h t)") for k in range(3)]
        Diag = set_buf[0].rearrange("p (e i) -> p e i", e=E)
        Block = set_buf[1].rearrange("p (e i) -> p e i", e=E)
        b_raw = set_buf[2][:, 0:2 * P].rearrange("p (n i) -> p n i", n=2)
        b_rest = set_buf[2][:, 2 * P:4 * P].rearrange("p (n i) -> p n i", n=2)
        xr = sp[:, 0, :].rearrange("p (j h) -> p j h", j=J)
        xn_p = sp[:, 1, :].rearrange("p (j h) -> p j h", j=J)
        dxs = y2[:, 0, :]
        t_rest = y2[0:3 * 2 * N, 1, :]

        G = [psum(f"G{b}", [P, CH]) for b in range(2)]
        PH = psum("PH", [P, CH])
        PY = psum("PY", [P, CH])
        PB = psum("PB", [P, CH])
        PC = psum("PC", [P, CH])
        Y = psum("Y", [P, HF, CH])
        Gb = [g[:, :].bitcast(BF16) for g in G]

        weights_in = sem("weights_in")
        zeroed = sem("zeroed")
        set_up = sem("set_up")
        a_exp = sem("a_exp")
        x_in = sem("x_in")
        x_final = sem("x_final")
        x_out = sem("x_out")
        g_full = [sem(f"g{b}_full") for b in range(2)]
        g_free = [sem(f"g{b}_free") for b in range(2)]
        names = ["f1", "f2", "p"]
        stats = [sem(f"stats_{w}") for w in names]
        moments = [sem(f"moments_{w}") for w in names]
        pool_ln = [sem(f"pool_ln_{w}") for w in names]
        scale_ready = [sem(f"scale_{w}") for w in names]
        normed = [sem(f"normed_{w}") for w in names]
        rms_normed = sem("rms_normed")
        residual = sem("residual")
        gate = [sem(f"gate_{w}") for w in names[:2]]
        pre_act = [sem(f"pre_act_{w}") for w in names[:2]]
        gelu = [sem(f"gelu_{w}") for w in names[:2]]
        w2_done = [sem(f"w2_done_{w}") for w in names[:2]]
        y_copied = [sem(f"y_copied_{w}") for w in names[:2]]
        conv = sem("conv")
        silu_x = sem("silu_x")
        t_part = sem("t_part")
        t_ready = sem("t_ready")
        relu = sem("relu")
        soft = sem("soft")
        dt_ready = sem("dt_ready")
        dtx_ready = sem("dtx_ready")
        decay = sem("decay")
        b_full = sem("b_full")
        c_full = sem("c_full")
        bx = sem("bx")
        scan = sem("scan")
        prod = sem("prod")
        paired = sem("paired")
        summed = sem("summed")
        yd = sem("yd")
        gated = sem("gated")

        loads = [(Win[:, :], winT), (Wx[:, :, :], wxT[:, 0:R].rearrange("(k p) m -> p k m", p=P)),
                 *[(Wbc[:, :, 2 * N * r:2 * N * (r + 1)], wxT[:, R:R + 2 * N].rearrange("(k p) m -> p k m", p=P))
                   for r in range(3)],
                 (Wdt[:, :], wdtT), (Wo[:, :, :], woT.rearrange("(k p) m -> p k m", p=P)),
                 (Wn[:, :], norm_w), (Wc[:, :, :], conv_w.rearrange("(k p) m -> p k m", p=P)),
                 (Bc[:, :], conv_b), (Bdt[:, :], dt_b),
                 (A[:, :, :], a_log.rearrange("(k p) m -> p k m", p=P)), (D[:, :], d_param),
                 (Wg[:, :], wg), (Bg[:, :], bg),
                 (W1[:, :, :], w1.rearrange("e h i -> h e i")), (W2[:, :, :], w2.rearrange("e i h -> i e h")),
                 *[(b_raw[E * r:E * (r + 1), n, :], b) for r in range(3) for n, b in enumerate((b1, b2))],
                 (Diag[:, :, :], diag), (Block[:, :, :], block), (Id[:, :], ident),
                 (Rank[:, :], rank), (Pick[:, :, :], pick)]
        N_ZERO = 7
        N_SET = 8

        blk = ctx.enter_context(nc.Block())

        @blk.sync
        def _(sp_):
            for dst, src in loads:
                sp_.dma_start(dst, src).then_inc(weights_in, 16)
            xd = x.rearrange("(t p) h -> p t h", p=P)
            od = out.rearrange("(t p) h -> p t h", p=P)
            sp_.dma_start(X[:, 0:J, :], xd[:, 0:J, :]).then_inc(x_in, 16)
            with sp_.Fori(1, NCH) as c:
                sp_.wait_ge(x_in, 16 * c)
                sp_.dma_start(X[:, bass.ds(J * c, J), :], xd[:, bass.ds(J * c, J), :]).then_inc(x_in, 16)
            with sp_.Fori(0, NCH) as c:
                sp_.wait_ge(x_in, 16 * NCH)
                sp_.wait_ge(x_final, c + 1)
                sp_.dma_start(od[:, bass.ds(J * c, J), :], X[:, bass.ds(J * c, J), :]).then_inc(x_out, 16)
            sp_.wait_ge(x_out, 16 * NCH)

        @blk.tensor
        def _(pe):
            pe.wait_ge(set_up, N_SET)
            pe.wait_ge(weights_in, 16 * len(loads))

            def transposes(it, name, src):
                b = G_AT[name][0]
                it.wait_free(pe, g_free, name)
                for j in range(J):
                    last = nc.tensor.transpose(G[b][:, P * j:P * (j + 1)], src(j), Id[:, :])
                last.then_inc(g_full[b], 1)

            def product(it, name, rows, terms, wait=True):
                b = G_AT[name][0]
                it.wait_free(pe, g_free, name)
                for k, (lhsT, rhs) in enumerate(terms):
                    last = nc.tensor.matmul(G[b][0:rows, :], lhsT, rhs, start=k == 0, stop=k == len(terms) - 1)
                last.then_inc(g_full[b], 1)

            def first_product(it, w, e):
                off = EXPERT[w]
                if e == 0:
                    pass
                    oh_use = f"oh_f{w + 1}"
                    before = Iteration(it.i0 - 1, it.turn)
                    before.wait_read(pe, g_free, oh_use)
                    if w == 1 and it.has(EXPERT[0]):
                        it.wait(pe, gelu[0], EXPERT[0], E, E)
                else:
                    it.wait(pe, gelu[w], off, E, e)
                nc.tensor.matmul(PH[:, :], Lm[:, e, :], ohT[:, w, :], start=True, stop=False)
                nc.tensor.matmul(PH[:, :], W1[:, e, :], xnT[:, w, :], start=False, stop=True) \
                    .then_inc(pre_act[w], 1)

            def second_product(it, w, e):
                off = EXPERT[w]
                it.wait(pe, gelu[w], off, E, e + 1)
                if e == 0:
                    if w == 0:
                        it.wait(pe, y_copied[1], -3, 1, 1)
                    elif it.i0 + 2 < NCH:
                        it.wait(pe, y_copied[0], 2, 1, 1)
                    else:
                        pe.wait_ge(y_copied[0], NCH)
                    nc.tensor.matmul(PY[:, :], b_part[:, 1, :], ohT[:, w, :], start=True, stop=False)
                nc.tensor.matmul(PY[:, :], W2[:, e, :], hs[:, e % 2, :], start=False, stop=e == E - 1) \
                    .then_inc(w2_done[w], 1)

            def y_transposes(it, w):
                it.wait(pe, y_copied[w], EXPERT[w], 1, 1)
                transposes(it, f"y_f{w + 1}", lambda j: yT[:, P * j:P * (j + 1)])

            def broadcast_b(it, off, n):
                c = (it.i0 + off) % 2
                if n == 0:
                    it.wait(pe, t_ready, off, 1, 1)
                it.wait(pe, bx, off, N, n)
                nc.tensor.matmul(PB[:, :], Pick[:, n, :], T3[:, c, :], start=True, stop=True).then_inc(b_full, 1)

            def broadcast_c(it, n):
                it.wait(pe, prod, 0, N, n)
                nc.tensor.matmul(PC[:, :], Pick[:, N + n, :], T3[:, it.i0 % 2, :], start=True, stop=True) \
                    .then_inc(c_full, 1)

            def sum_pair(it, off, q):
                if q == 0:
                    it.wait(pe, yd, off, HF, 0)
                it.wait(pe, paired, off, N // 2, q + 1)
                for h in range(HF):
                    last = nc.tensor.matmul(Y[:, h, :], Id[:, :], pair[:, q % 2, h, :],
                                            start=q == 0, stop=q == N // 2 - 1)
                last.then_inc(summed, 1)

            def body(it):
                waiting = []
                for s in range(SLOTS):
                    if it.has(0):
                        broadcast_c(it, s)
                        if s < N - 1:
                            broadcast_b(it, 0, s + 1)
                    if s == N - 1 and it.has(1):
                        broadcast_b(it, 1, 0)
                    for w, e in slot_units(s):
                        if it.has(EXPERT[w]):
                            first_product(it, w, e)
                            waiting.append((w, e))
                        while len(waiting) > 1:
                            second_product(it, *waiting.pop(0))
                    if not slot_units(s) or (0, E - 1) in waiting and not it.has(EXPERT[1]):
                        while waiting:
                            second_product(it, *waiting.pop(0))
                    if s == 1 and it.has(-1):
                        sum_pair(it, -1, N // 2 - 1)
                    if s % 2 and s > 1 and it.has(0):
                        sum_pair(it, 0, (s - 3) // 2)
                    c = (it.i0 + 1) % 2
                    if s == 2 and it.has(1):
                        it.wait(pe, rms_normed, 1, 1, 1)
                        transposes(it, "ln_p", lambda j: xr[:, j, :])
                    if s == 3 and it.has(-1):
                        it.wait(pe, gated, -1, 1, 1)
                        it.wait_free(pe, g_free, "out")
                        for j in range(J):
                            for h in range(HF):
                                last = nc.tensor.matmul(G[0][:, P * j:P * (j + 1)], y2[:, h, P * j:P * (j + 1)],
                                                        Wo[:, h, :], start=h == 0, stop=h == HF - 1)
                        last.then_inc(g_full[0], 1)
                    if s == 3 and it.has(1):
                        it.wait_read(pe, g_free, "ln_p")
                        product(it, "x1", P, [(Win[:, P:2 * P], xrT[:, :])])
                    if s == 4 and it.has(1):
                        product(it, "x0", P, [(Win[:, 0:P], xrT[:, :])])
                    if s == 5 and it.has(1):
                        product(it, "z0", P, [(Win[:, 2 * P:3 * P], xrT[:, :])])
                        product(it, "z1", P, [(Win[:, 3 * P:4 * P], xrT[:, :])])
                    if s == 8 and it.has(1):
                        it.wait(pe, silu_x, 1, 1, 1)
                        xsc = xs[:, c].rearrange("p h b l -> p h (b l)")
                        product(it, "dtx", P, [(Wx[:, h, :], xsc[:, h, :]) for h in range(HF)])
                        product(it, "bc", 3 * 2 * N, [(Wbc[:, h, :], xsc[:, h, :]) for h in range(HF)])
                    if s == 9 and it.has(2):
                        y_transposes(it, 0)
                    if s == 9 and it.has(1):
                        it.wait_read(pe, g_free, "dtx")
                        for h in range(HF):
                            product(it, f"dt{h}", P, [(Wdt[:, P * h:P * (h + 1)], dxs[:, :])])
                    if s == 11 and it.has(-2):
                        y_transposes(it, 1)
                    for w in range(2):
                        if s == 12 and it.has(FRONT[w]):
                            it.wait(pe, normed[w], FRONT[w], 1, 1)
                            transposes(it, f"ln_f{w + 1}", lambda j: xn[:, w, j, :])
                    for w in range(2):
                        if s == 13 and it.has(FRONT[w]):
                            name = f"gate_f{w + 1}"
                            b = G_AT[name][0]
                            it.wait_read(pe, g_free, f"ln_f{w + 1}")
                            for j in range(J):
                                last = nc.tensor.matmul(G[b][:, E * j:E * (j + 1)], xnT[:, w, P * j:P * (j + 1)],
                                                        Wg[:, :], start=True, stop=True)
                            last.then_inc(g_full[b], 1)
                    for w in range(2):
                        if s == 15 and it.has(FRONT[w]):
                            name = f"oh_f{w + 1}"
                            b = G_AT[name][0]
                            it.wait(pe, gate[w], FRONT[w], 5, 5)
                            it.wait_free(pe, g_free, name)
                            for j in range(J):
                                last = nc.tensor.transpose(Gb[b][0:3 * E, P * j:P * (j + 1)],
                                                           oh[:, w, j].rearrange("p r e -> p (r e)"), Idb[:, :])
                            last.then_inc(g_full[b], 1)

            schedule(pe, body)

        @blk.scalar
        def _(act):
            act.wait_ge(weights_in, 16 * len(loads))
            nc.scalar.activation(A[:, :, :], A[:, :, :], ACT.Exp).then_inc(a_exp, 1)
            act.wait_ge(set_up, N_SET)
            act.wait_ge(zeroed, N_ZERO)

            def copy_out(it, name, dst, rows=P):
                b = G_AT[name][0]
                it.wait_full(act, g_full, name)
                nc.scalar.copy(dst, G[b][0:rows, :]).then_inc(g_free[b], 1)

            def y_copy(it, w):
                off = EXPERT[w]
                it.wait(act, w2_done[w], off, E, E)
                if w == 1 and it.has(2):
                    it.wait_full(act, g_full, "y_f1")
                if w == 0 and it.has(-3):
                    Iteration(it.i0 - 1, it.turn).wait_full(act, g_full, "y_f2")
                if w == 1 and not it.has(2) and it.has(-3):
                    Iteration(it.i0 - 1, it.turn).wait_full(act, g_full, "y_f2")
                if w == 0 and not it.has(-3) and it.has(1):
                    Iteration(it.i0 - 1, it.turn).wait_full(act, g_full, "y_f1")
                nc.scalar.copy(yT[:, :], PY[:, :]).then_inc(y_copied[w], 1)

            def decays(it, states):
                for n in states:
                    it.wait(act, scan, 0, N, n + 1)
                    for h in range(HF):
                        nc.scalar.activation(dA[:, n, h, :, 1:L], dt[:, h, :, 1:L], ACT.Exp,
                                             scale=A[:, h, n:n + 1]).then_inc(decay, 1)

            def body(it):
                c = (it.i0 + 1) % 2
                for s in range(SLOTS):
                    for w, e in slot_units(s):
                        if it.has(EXPERT[w]):
                            if e >= 2:
                                it.wait(act, w2_done[w], EXPERT[w], E, e - 1)
                            it.wait(act, pre_act[w], EXPERT[w], E, e + 1)
                            nc.scalar.activation(hs[:, e % 2, :], PH[:, :], ACT.Gelu).then_inc(gelu[w], 1)
                            if w == 1 and e == 1 and it.has(EXPERT[0]):
                                y_copy(it, 0)
                    if s == 7 and it.has(EXPERT[0]) and not it.has(EXPERT[1]):
                        y_copy(it, 0)
                    if s == 2 and it.has(1):
                        copy_out(it, "ln_p", xrT[:, :])
                    if it.has(1) and s in (3, 4):
                        h = 4 - s
                        b = h
                        it.wait(act, conv, 1, 2 * (K - 1), 0)
                        it.wait(act, yd, -1, HF, HF)
                        it.wait_full(act, g_full, f"x{h}")
                        src = G[b][:, :].rearrange("p (b l) -> p b l", b=NB)
                        nc.scalar.copy(xp[:, h, :, K - 1:K - 1 + L], src)
                        nc.scalar.activation(xs[:, c, h], src, ACT.Identity, scale=Wc[:, h, K - 1:K],
                                             bias=Bc[:, h:h + 1]).then_inc(g_free[b], 1)
                    if s == 7 and it.has(1):
                        it.wait(act, gated, -1, 1, 1)
                        for h in range(HF):
                            it.wait_full(act, g_full, f"z{h}")
                            nc.scalar.activation(zs[:, c, h, :], G[h][:, :], ACT.Silu).then_inc(g_free[h], 1)
                        it.wait(act, conv, 1, 2 * (K - 1), 2 * (K - 1))
                        nc.scalar.activation(xs[:, c], xs[:, c], ACT.Silu).then_inc(silu_x, 1)
                    if s == 8 and it.has(1):
                        if it.has(-1):
                            it.wait_full(act, g_full, "out")
                        copy_out(it, "dtx", dxs[:, :])
                        it.wait(act, prod, -1, N, N)
                        it.wait_full(act, g_full, "bc")
                        nc.scalar.copy(T3[:, c, :], G[1][0:3 * 2 * N, :]).then_inc(t_part, 1)
                        it.wait_read(act, g_free, "bc")
                        nc.scalar.copy(T3[0:2 * 2 * N, c, :], t_rest[0:2 * 2 * N, :]).then_inc(t_part, 1)
                    if s == 10 and it.has(1):
                        it.wait(act, residual, 1, 1, 1)
                        for h in range(HF):
                            it.wait(act, relu, 1, HF, h + 1)
                            nc.scalar.activation(sp[:, h, :], G[h][:, :], ACT.Abs, bias=Bdt[:, h:h + 1]) \
                                .then_inc(g_free[h], 1)
                    if s == 11 and it.has(EXPERT[1]):
                        y_copy(it, 1)
                    if s == 11 and it.has(1):
                        for h in range(HF):
                            it.wait_read(act, g_free, f"dt{h}")
                        nc.scalar.activation(sp[:, :, :], sp[:, :, :], ACT.Exp, scale=-1.0).then_inc(soft, 1)
                        it.wait(act, soft, 1, 2, 1)
                        nc.scalar.activation(sp[:, :, :], sp[:, :, :], ACT.Ln, bias=1.0).then_inc(soft, 1)
                    for w in range(2):
                        if s == 12 and it.has(FRONT[w]):
                            copy_out(it, f"ln_f{w + 1}", xnT[:, w, :])
                    if s == 13 and it.has(1):
                        it.wait(act, dt_ready, 1, 1, 1)
                    if it.has(1) and s >= 13:
                        decays(it, {13: range(0, 5), 14: range(5, 10), 15: range(10, N)}[s])

            schedule(act, body)

        @blk.vector
        def _(dve):
            nc.vector.memset(dA[:, :, :, :, 0:1], 0.0).then_inc(zeroed, 1)
            nc.vector.memset(xp[:, :, :, 0:K - 1], 0.0).then_inc(zeroed, 1)
            nc.vector.memset(half[:, :], -0.5).then_inc(zeroed, 1)
            nc.vector.memset(eps[:, 0], LN_EPS).then_inc(zeroed, 1)
            nc.vector.memset(eps[:, 1], RMS_EPS).then_inc(zeroed, 1)
            nc.vector.memset(ticket[:, 0:1], 0.0).then_inc(zeroed, 1)
            dve.wait_ge(weights_in, 16 * len(loads))
            nc.vector.tensor_copy(Idb[:, :], Id[:, :]).then_inc(zeroed, 1)
            dve.wait_ge(a_exp, 1)
            nc.vector.tensor_scalar(A[:, :, :], A[:, :, :], -1.0, None, ALU.mult).then_inc(set_up, 1)
            nc.vector.tensor_scalar(Win[:, :], Win[:, :], Wn[:, 0:1], None, ALU.mult).then_inc(set_up, 1)
            nc.vector.tensor_copy(b_part[:, :, :], b_raw[:, :, :]).then_inc(set_up, 1)
            dve.wait_ge(set_up, 3)
            nc.vector.tensor_tensor(b_rest[0:2 * E], b_raw[0:2 * E], b_part[0:2 * E], ALU.subtract).then_inc(set_up, 1)
            dve.wait_ge(set_up, 4)
            nc.vector.tensor_copy(b_part[0:2 * E], b_rest[0:2 * E]).then_inc(set_up, 1)
            dve.wait_ge(set_up, 5)
            nc.vector.tensor_tensor(b_part[0:E], b_rest[0:E], b_part[0:E], ALU.subtract).then_inc(set_up, 1)
            dve.wait_ge(set_up, 6)
            nc.vector.tensor_tensor(Diag[:, :, :], Diag[:, :, :],
                                    b_part[:, 0:1, :].broadcast_to([3 * E, E, P]), ALU.mult).then_inc(set_up, 1)
            dve.wait_ge(set_up, 7)
            nc.vector.tensor_tensor(Lm[:, :, :], Diag[:, :, :], Block[:, :, :], ALU.add).then_inc(set_up, 1)
            dve.wait_ge(set_up, N_SET)
            dve.wait_ge(zeroed, N_ZERO)

            def norm_stats(it, w, off):
                if w == 0:
                    dve.wait_ge(set_up, N_SET)
                    it.wait(dve, x_in, off, 16, 16)
                for j in range(J):
                    last = nc.vector.bn_stats(stat[:, w, j, :], X[:, it.tiles(off, j, 1), :])
                last.then_inc(stats[w], 1)
                it.wait(dve, stats[w], off, 1, 1)
                it.wait(dve, scale_ready[w], off, 1, 0)
                nc.vector.tensor_copy(ticket[:, 1:2], ticket[:, 0:1])
                for j in range(J):
                    last = nc.vector.bn_aggr(mv[:, w, j, :], stat[:, w, j, :])
                last.then_inc(moments[w], 1)

            def normalize(it, w, off, dst, scale, done):
                for j in range(J):
                    last = nc.vector.tensor_scalar(dst[:, j:j + 1, :], X[:, it.tiles(off, j, 1), :],
                                                   mv[:, w, j, 0:1], scale[:, j:j + 1], ALU.subtract, ALU.mult)
                last.then_inc(done, 1)

            def state_bx(it, off, n):
                c = (it.i0 + off) % 2
                if n == 0:
                    it.wait(dve, dtx_ready, off, 1, 1)
                it.wait(dve, b_full, off, N, n + 1)
                it.wait(dve, paired, off, N // 2, (n - 4) // 2 + 1)
                nc.vector.tensor_tensor(hb[:, n % 4], dtx[:, c], PB[:, None, :].broadcast_to([P, HF, CH]),
                                        ALU.mult).then_inc(bx, 1)

            def state_scan(it, n):
                it.wait(dve, decay, 0, HF * N, HF * (n + 1))
                it.wait(dve, bx, 0, N, n + 1)
                h = hb[:, n % 4].rearrange("p h t -> p (h t)")
                nc.vector.tensor_tensor_scan(h, dA[:, n].rearrange("p h b l -> p (h b l)"), h, 0.0,
                                             ALU.mult, ALU.add).then_inc(scan, 1)

            def state_prod(it, n):
                it.wait(dve, c_full, 0, N, n + 1)
                it.wait(dve, scan, 0, N, n + 1)
                nc.vector.tensor_tensor(hb[:, n % 4], hb[:, n % 4], PC[:, None, :].broadcast_to([P, HF, CH]),
                                        ALU.mult).then_inc(prod, 1)

            def convolve(it, k):
                c = (it.i0 + 1) % 2
                for h in (1, 0):
                    if k == 0:
                        it.wait_read(dve, g_free, f"x{h}")
                    else:
                        it.wait(dve, conv, 1, 2 * (K - 1), 2 * k - h)
                    nc.vector.scalar_tensor_tensor(xs[:, c, h], xp[:, h, :, k:k + L], Wc[:, h, k:k + 1],
                                                   xs[:, c, h], ALU.mult, ALU.add).then_inc(conv, 1)

            def one_hot(it, w):
                off, name = FRONT[w], f"gate_f{w + 1}"
                b = G_AT[name][0]
                it.wait_full(dve, g_full, name)
                nc.vector.tensor_tensor(lg[:, w].rearrange("p j e -> p (j e)"), G[b][:, 0:J * E], Bg[:, :],
                                        ALU.add).then_inc(g_free[b], 1)
                it.wait_read(dve, g_free, name)
                nc.vector.tensor_reduce(mx[:, w, 0], lg[:, w], AX_X, ALU.max).then_inc(gate[w], 1)
                it.wait(dve, gate[w], off, 5, 1)
                nc.vector.tensor_tensor(eq[:, w], lg[:, w], mx[:, w, 0, :, None].broadcast_to([P, J, E]),
                                        ALU.is_ge).then_inc(gate[w], 1)
                it.wait(dve, gate[w], off, 5, 2)
                nc.vector.tensor_tensor(eq[:, w], eq[:, w], Rank[:, :].rearrange("p (j e) -> p j e", j=J),
                                        ALU.mult).then_inc(gate[w], 1)
                it.wait(dve, gate[w], off, 5, 3)
                nc.vector.tensor_reduce(mx[:, w, 1], eq[:, w], AX_X, ALU.max).then_inc(gate[w], 1)
                it.wait(dve, gate[w], off, 5, 4)
                nc.vector.tensor_tensor(oh[:, w], eq[:, w, :, None, :].broadcast_to([P, J, 3, E]),
                                        mx[:, w, 1, :, None, None].broadcast_to([P, J, 3, E]),
                                        ALU.is_equal).then_inc(gate[w], 1)

            def one_hot_out(it, w):
                name = f"oh_f{w + 1}"
                b = G_AT[name][0]
                it.wait_full(dve, g_full, name)
                nc.vector.tensor_copy(ohT[:, w, :], Gb[b][0:3 * E, 0:CH]).then_inc(g_free[b], 1)

            def add_to_x(it, name, off, scale):
                b = G_AT[name][0]
                it.wait_full(dve, g_full, name)
                xc = X[:, it.tiles(off), :]
                nc.vector.scalar_tensor_tensor(xc, G[b][:, :].rearrange("p (j h) -> p j h", j=J), scale, xc,
                                               ALU.mult, ALU.add).then_inc(g_free[b], 1)

            def body(it):
                c = (it.i0 + 1) % 2
                for s in range(SLOTS):
                    if it.has(0):
                        state_scan(it, s)
                        if s < N - 1:
                            state_bx(it, 0, s + 1)
                        state_prod(it, s)
                    if s == 0 and it.has(1):
                        dve.wait_ge(set_up, N_SET)
                        Iteration(it.i0 - 1, it.turn).wait_read(dve, g_free, "y_f1")
                        norm_stats(it, 2, 1)
                    if s == 1 and it.has(1):
                        it.wait(dve, scale_ready[2], 1, 1, 1)
                        normalize(it, 2, 1, xr, rms[:, 1], rms_normed)
                        normalize(it, 2, 1, xn_p, rstd[:, 2], normed[2])
                    if s == 2 and it.has(-1):
                        it.wait(dve, summed, -1, N // 2, N // 2)
                        cc = (it.i0 - 1) % 2
                        for h in range(HF):
                            nc.vector.scalar_tensor_tensor(
                                y2[:, h, :], xs[:, cc, h].rearrange("p b l -> p (b l)"), D[:, h:h + 1], Y[:, h, :],
                                ALU.mult, ALU.add).then_inc(yd, 1)
                    if s == 4 and it.has(-1):
                        it.wait(dve, residual, -1, 1, 1)
                        add_to_x(it, "out", -1, 1.0)
                    if s in (5, 6) and it.has(1):
                        for k in {5: (0, 1), 6: (2,)}[s]:
                            convolve(it, k)
                    if s == 8 and it.has(1):
                        it.wait(dve, t_part, 1, 2, 1)
                        nc.vector.tensor_tensor(t_rest[:, :], G[1][0:3 * 2 * N, :], T3[:, c, :],
                                                ALU.subtract).then_inc(g_free[1], 1)
                        it.wait(dve, t_part, 1, 2, 2)
                        nc.vector.tensor_tensor(T3[0:2 * N, c, :], t_rest[0:2 * N, :], T3[0:2 * N, c, :],
                                                ALU.subtract).then_inc(t_ready, 1)
                    if s == 9 and it.has(2):
                        add_to_x(it, "y_f1", 2, 0.5)
                    if s == 9 and it.has(3):
                        norm_stats(it, 0, 3)
                    if s == 10 and it.has(1):
                        it.wait(dve, decay, 0, HF * N, HF * N)
                        for h in range(HF):
                            it.wait_full(dve, g_full, f"dt{h}")
                            nc.vector.tensor_scalar(dt[:, h].rearrange("p b l -> p (b l)"), G[h][:, :],
                                                    Bdt[:, h:h + 1], 0.0, ALU.add, ALU.max).then_inc(relu, 1)
                    if s == 10 and it.has(-1):
                        dve.wait_ge(set_up, N_SET)
                        it.wait_read(dve, g_free, "out")
                        norm_stats(it, 1, -1)
                    if s == 11:
                        for w in range(2):
                            if it.has(FRONT[w]):
                                it.wait(dve, scale_ready[w], FRONT[w], 1, 1)
                                normalize(it, w, FRONT[w], xn[:, w], rstd[:, w], normed[w])
                    if s == 12 and it.has(-2):
                        b = G_AT["y_f2"][0]
                        it.wait_full(dve, g_full, "y_f2")
                        add_to_x(it, "y_f2", -2, 0.5)
                    if s == 13 and it.has(-2):
                        it.wait_read(dve, g_free, "y_f2")
                        dve.sem_inc(x_final, 1)
                    if s == 14:
                        for w in range(2):
                            if it.has(FRONT[w]):
                                one_hot(it, w)
                    if s == N - 1:
                        for w in range(2):
                            if it.has(FRONT[w]):
                                one_hot_out(it, w)
                        if it.has(1):
                            state_bx(it, 1, 0)

            schedule(dve, body)

        @blk.gpsimd
        def _(pool):
            pool.wait_ge(zeroed, N_ZERO)

            def inverse_root(it, w, off):
                m = 5 if w == 2 else 1
                it.wait(pool, moments[w], off, 1, 1)
                nc.gpsimd.tensor_tensor(vt[:, w, :], mv[:, w, :, 1], eps[:, 0], ALU.add).then_inc(pool_ln[w], 1)
                it.wait(pool, pool_ln[w], off, m, 1)
                it.wait(pool, normed[w], off, 1, 0)
                last = nc.gpsimd.tensor_tensor(rstd[:, w, :], vt[:, w, :], half[:, 0:J], ALU.pow)
                if w < 2:
                    last.then_inc(scale_ready[w], 1)
                    return
                last.then_inc(pool_ln[w], 1)
                it.wait(pool, pool_ln[w], off, m, 2)
                nc.gpsimd.tensor_tensor(vt[:, w, :], rstd[:, w, :], rstd[:, w, :], ALU.mult).then_inc(pool_ln[w], 1)
                it.wait(pool, pool_ln[w], off, m, 3)
                nc.gpsimd.tensor_tensor(vt[:, w, :], vt[:, w, :], mv[:, w, :, 1], ALU.mult).then_inc(pool_ln[w], 1)
                it.wait(pool, pool_ln[w], off, m, 4)
                nc.gpsimd.tensor_tensor(vt[:, w, :], vt[:, w, :], eps[:, 1], ALU.add).then_inc(pool_ln[w], 1)
                it.wait(pool, pool_ln[w], off, m, 5)
                nc.gpsimd.tensor_tensor(rms[:, 0], vt[:, w, :], half[:, 0:J], ALU.pow).then_inc(rms_root, 1)
                it.wait(pool, rms_root, off, 1, 1)
                nc.gpsimd.tensor_tensor(rms[:, 1], rms[:, 0], rstd[:, w, :], ALU.mult).then_inc(scale_ready[w], 1)

            def add_pair(it, off, q):
                it.wait(pool, prod, off, N, 2 * q + 2)
                it.wait(pool, summed, off, N // 2, q - 1)
                a = 2 * q % 4
                nc.gpsimd.tensor_tensor(pair[:, q % 2], hb[:, a], hb[:, a + 1], ALU.add).then_inc(paired, 1)

            def body(it):
                c = (it.i0 + 1) % 2
                for s in range(SLOTS):
                    if s == 0 and it.has(-1):
                        add_pair(it, -1, N // 2 - 1)
                    if s % 2 == 0 and s > 0 and it.has(0):
                        add_pair(it, 0, s // 2 - 1)
                    if s == 0 and it.has(1):
                        inverse_root(it, 2, 1)
                    if s == 1 and it.has(1):
                        it.wait(pool, normed[2], 1, 1, 1)
                        xc = X[:, it.tiles(1), :]
                        nc.gpsimd.tensor_tensor(xc, xc, xn_p, ALU.add).then_inc(residual, 1)
                    if s == 2 and it.has(-1):
                        cc = (it.i0 - 1) % 2
                        it.wait(pool, yd, -1, HF, HF)
                        nc.gpsimd.tensor_tensor(y2[:, :, :], y2[:, :, :], zs[:, cc], ALU.mult).then_inc(gated, 1)
                    if s == 9 and it.has(3):
                        inverse_root(it, 0, 3)
                    if s == 10 and it.has(-1):
                        inverse_root(it, 1, -1)
                    if s == 12 and it.has(1):
                        it.wait(pool, soft, 1, 2, 2)
                        d = dt[:, :, :, :].rearrange("p h b l -> p h (b l)")
                        nc.gpsimd.tensor_tensor(d, d, sp[:, :, :], ALU.add).then_inc(dt_ready, 1)
                        it.wait(pool, dt_ready, 1, 1, 1)
                        it.wait(pool, bx, -1, N, N)
                        nc.gpsimd.tensor_tensor(dtx[:, c], d, xs[:, c].rearrange("p h b l -> p h (b l)"),
                                                ALU.mult).then_inc(dtx_ready, 1)

            rms_root = ctx.enter_context(nc.semaphore("rms_root"))
            schedule(pool, body)



def kernel(**inputs):
    import concourse.bacc as _bacc
    import ml_dtypes as _ml
    from concourse.bass_utils import run_bass_kernel_spmd as _run

    v = {k: np.asarray(a) for k, a in inputs.items()}
    flat = np.ascontiguousarray
    x = v["L0_attn_x"]

    def halves(a):
        return flat(a.reshape(HF, P).T)

    rank = np.tile(np.arange(E, 0, -1, dtype=np.float32), (P, J))
    pick = np.zeros((3, 2 * N, 2 * N, P), _ml.bfloat16)
    diag = np.zeros((3, E, E, P), np.float32)
    block = np.zeros((3, E, E, P), np.float32)
    for n in range(2 * N):
        pick[:, n, n, :] = 1.0
    for e in range(E):
        diag[:, e, e, :] = 1.0
        block[2, e, :, :] = -BIG
        block[2, e, e, :] = 0.0
    arrays = {
        "x": flat(x.reshape(NTOK, H)),
        "winT": flat(v["L0_attn_in_proj_w"].T), "wxT": flat(v["L0_attn_x_proj_w"].T),
        "wdtT": flat(v["L0_attn_dt_proj_w"].T), "woT": flat(v["L0_attn_out_proj_w"].T),
        "norm_w": flat(v["L0_attn_norm_w"].reshape(P, 1)),
        "conv_w": flat(v["L0_attn_conv_w"].reshape(DI, K)), "conv_b": halves(v["L0_attn_conv_b"]),
        "dt_b": halves(v["L0_attn_dt_proj_b"]), "a_log": flat(v["L0_attn_A_log"]),
        "d_param": halves(v["L0_attn_D_param"]),
        "wg": flat(v["L0_ffn_Wg"]), "bg": flat(np.tile(v["L0_ffn_bg"], (P, J))),
        "w1": flat(v["L0_ffn_W1"]), "b1": flat(v["L0_ffn_b1"]),
        "w2": flat(v["L0_ffn_W2"]), "b2": flat(v["L0_ffn_b2"]),
        "ident": np.eye(P, dtype=np.float32), "rank": rank,
        "pick": pick.reshape(3 * 2 * N, 2 * N, P), "diag": diag.reshape(3 * E, E, P),
        "block": block.reshape(3 * E, E, P),
    }
    nc = _bacc.Bacc("TRN2", target_bir_lowering=False, num_devices=1)
    args = [nc.dram_tensor(f"in_{k}", a.shape, mybir.dt.from_np(a.dtype), kind="ExternalInput").ap()
            for k, a in arrays.items()]
    out = nc.dram_tensor("out_0", (NTOK, H), F32, kind="ExternalOutput").ap()
    macaron_kernel(nc, *args, out)
    r = _run(nc, [{f"in_{k}": a for k, a in arrays.items()}], core_ids=[0])
    return r.results[0]["out_0"].reshape(x.shape)
```

```python
from contextlib import ExitStack

import concourse.bass as bass
import numpy as np
from concourse import mybir

F32 = mybir.dt.float32
BF16 = mybir.dt.bfloat16
ALU = mybir.AluOpType
ACT = mybir.ActivationFunctionType
AX_X = mybir.AxisListType.X

P = 128
H = 128
L = 256
NTOK = 32 * L
CH = 2 * L
NB = CH // L
J = CH // P
NCH = NTOK // CH
DI = 256
HF = DI // P
N = 16
SLOTS = N
K = 4
R = 128
E = 8
BIG = 1.0e30
XR = 8
HR = 8
LN_EPS, RMS_EPS = 1e-5, 1e-6

FIRST, LAST = -3, NCH + 1
LOOP0, LOOP1 = 3, NCH - 3

G_SEQ = [("oh_f1", 1, 2), ("oh_f2", 0, -2), ("x1", 1, 1), ("x0", 0, 1), ("z0", 0, 1), ("z1", 1, 1),
         ("dtx", 0, 1), ("out", 1, -1), ("y_f1", 0, 2), ("bc", 1, 1), ("dt0", 0, 1), ("dt1", 0, 1),
         ("ln_f1", 1, 3), ("gate_f1", 1, 3), ("y_f2", 0, -2), ("ln_f2", 1, -1), ("gate_f2", 1, -1),
         ("ln_p", 0, 2)]
G_AT = {name: (bank, off) for name, bank, off in G_SEQ}
UNITS = [0, 1, 2, 1, 2, 2, 1, 2, 2, 1, 2, 0, 0, 0, 0, 0]
assert sum(UNITS) == 2 * E
POOL_C = (2, 4, 6, 8, 10, 12, 14)
DR = 12
DECAYS = [0, 1, 2, 3, 8, 9, 10, 11, 4, 5, 6, 7, 12, 13, 14, 15]
DA_AT = [n if n < DR else n - 8 for n in range(N)]
RC = 4
Q = 4
FRONT = {0: 3, 1: -1}
EXPERT = {0: 2, 1: -2}


def g_uses(i, name):
    bank = G_AT[name][0]
    n = sum(0 <= k + off < NCH for k in range(FIRST, i) for _, b, off in G_SEQ if b == bank)
    for other, b, off in G_SEQ:
        if other == name:
            return n
        n += b == bank and 0 <= i + off < NCH


G_EACH = [sum(b == bank for _, b, _ in G_SEQ) for bank in range(2)]


class Iteration:

    def __init__(self, i0, turn=None):
        self.i0, self.turn = i0, turn

    def value(self, at_i0, each):
        return at_i0 if self.turn is None else at_i0 + 2 * each * self.turn

    def has(self, off):
        return 0 <= self.i0 + off < NCH

    def wait(self, eng, sem, off, each, k):
        n = each * (self.i0 + off) + k
        if n > 0:
            eng.wait_ge(sem, self.value(n, each))

    def wait_full(self, eng, g_full, name):
        bank = G_AT[name][0]
        eng.wait_ge(g_full[bank], self.value(g_uses(self.i0, name) + 1, G_EACH[bank]))

    def wait_read(self, eng, g_free, name):
        bank = G_AT[name][0]
        eng.wait_ge(g_free[bank], self.value(g_uses(self.i0, name) + 1, G_EACH[bank]))

    def wait_free(self, eng, g_free, name):
        bank, n = G_AT[name][0], g_uses(self.i0, name)
        if n > 0:
            eng.wait_ge(g_free[bank], self.value(n, G_EACH[bank]))

    def before(self):
        return Iteration(self.i0 - 1, self.turn)

    def tiles(self, off, j=0, n=J):
        return bass.ds(self.value(J * (self.i0 + off) + j, J) % (J * XR), n)


def schedule(eng, body):
    for i in range(FIRST, LOOP0):
        body(Iteration(i))
    with eng.Fori(0, (LOOP1 - LOOP0) // 2) as turn:
        body(Iteration(LOOP0, turn))
        body(Iteration(LOOP0 + 1, turn))
    for i in range(LOOP0 + (LOOP1 - LOOP0) // 2 * 2, LAST + 1):
        body(Iteration(i))


def on_pool(n):
    return sum(m in POOL_C for m in range(n))


NP, NV = on_pool(N), N - on_pool(N)


def slot_units(s):
    at = sum(UNITS[:s])
    return [(u // E, u % E) for u in range(at, at + UNITS[s])]


def macaron_kernel(nc, x, winT, wxT, wdtT, woT, norm_w, conv_w, conv_b, dt_b, a_log, d_param,
                   wg, bg, w1, b1, w2, b2, ident, rank, pick, diag, block, c_dram, out):
    with ExitStack() as ctx:
        def sb(name, shape, dt=F32):
            return ctx.enter_context(nc.sbuf_tensor(name, shape, dt))

        def psum(name, shape):
            return ctx.enter_context(nc.psum_tensor(name, shape, F32))

        def sem(name):
            return ctx.enter_context(nc.semaphore(name))

        X = sb("X", [P, XR * J, H])
        Win = sb("Win", [P, 2 * DI])
        Wx = sb("Wx", [P, HF, R])
        Wbc = sb("Wbc", [P, HF, 3 * 2 * N])
        Wdt = sb("Wdt", [P, DI])
        Wo = sb("Wo", [P, HF, H])
        Wn = sb("Wn", [P, 1])
        Wc = sb("Wc", [P, HF, K])
        Bc = sb("Bc", [P, HF])
        Bdt = sb("Bdt", [P, HF])
        A = sb("A", [P, HF, N])
        D = sb("D", [P, HF])
        Dd = sb("Dd", [P, HF, P])
        Wg = sb("Wg", [P, E])
        Bg = sb("Bg", [P, J * E])
        W1 = sb("W1", [P, E, P])
        W2 = sb("W2", [P, E, H])
        b_part = sb("b_part", [3 * E, 2, P], BF16)
        Lm = sb("Lm", [3 * E, E, P], BF16)
        Id = sb("Id", [P, P])
        Idb = sb("Idb", [P, P], BF16)
        Rank = sb("Rank", [P, J * E])
        Pick = sb("Pick", [3 * 2 * N, 2 * N], BF16)
        ticket = sb("ticket", [P, 2])
        eps = sb("eps", [P, 2, J])
        half = sb("half", [P, 2 * J])
        stat = sb("stat", [P, 3, J, 6])
        mv = sb("mv", [P, 3, J, 2])
        vt = sb("vt", [P, 3, J])
        rstd = sb("rstd", [P, 3, J])
        rms = sb("rms", [P, 2, J])
        xn = sb("xn", [P, 2, J, H])
        xnT = sb("xnT", [P, 2, CH])
        lg = sb("lg", [P, 2, J, E])
        eq = sb("eq", [P, 2, J, E])
        mx = sb("mx", [P, 2, 2, J])
        oh = sb("oh", [P, 2, J, 3, E], BF16)
        ohT = sb("ohT", [3 * E, 2, CH], BF16)
        hs = sb("hs", [P, 2, CH])
        yT = sb("yT", [P, CH])
        xrT = yT
        xp = sb("xp", [P, HF, NB, K - 1 + L])
        xs = sb("xs", [P, 2, HF, NB, L])
        zs = sb("zs", [P, 2, HF, CH])
        T3 = sb("T3", [3 * 2 * N, 2, CH], BF16)
        sp = sb("sp", [P, HF, CH])
        dt = sb("dt", [P, 2, HF, NB, L])
        dtx = sb("dtx", [P, 2, HF, CH])
        dA = sb("dA", [P, DR, HF, NB, L])
        hb = sb("hb", [P, HR, HF, CH])
        pair = sb("pair", [P, 3, HF, CH])
        cs = sb("cs", [P, RC, CH])
        bcT = sb("bcT", [2 * N, CH])
        y2 = sb("y2", [P, HF, CH])
        set_buf = [hb[0:3 * E, k].rearrange("p h t -> p (h t)") for k in range(3)]
        Diag = set_buf[0].rearrange("p (e i) -> p e i", e=E)
        Block = set_buf[1].rearrange("p (e i) -> p e i", e=E)
        b_raw = set_buf[2][:, 0:2 * P].rearrange("p (n i) -> p n i", n=2)
        b_rest = set_buf[2][:, 2 * P:4 * P].rearrange("p (n i) -> p n i", n=2)
        xr = sp[:, 0, :].rearrange("p (j h) -> p j h", j=J)
        xn_p = sp[:, 1, :].rearrange("p (j h) -> p j h", j=J)
        dxs = y2[:, 0, :]
        t_rest = y2[0:3 * 2 * N, 1, :]

        G = [psum(f"G{b}", [P, CH]) for b in range(2)]
        PH = psum("PH", [P, CH])
        PY = psum("PY", [P, CH])
        PB = [psum(f"PB{k}", [P, CH]) for k in range(2)]
        Y = psum("Y", [P, HF, CH])
        Gb = [g[:, :].bitcast(BF16) for g in G]

        weights_in = sem("weights_in")
        zeroed = sem("zeroed")
        set_up = sem("set_up")
        a_exp = sem("a_exp")
        x_in = sem("x_in")
        x_final = sem("x_final")
        x_out = sem("x_out")
        g_full = [sem(f"g{b}_full") for b in range(2)]
        g_free = [sem(f"g{b}_free") for b in range(2)]
        names = ["f1", "f2", "p"]
        stats = [sem(f"stats_{w}") for w in names]
        moments = [sem(f"moments_{w}") for w in names]
        pool_ln = [sem(f"pool_ln_{w}") for w in names]
        scale_ready = [sem(f"scale_{w}") for w in names]
        normed = [sem(f"normed_{w}") for w in names]
        rms_normed = sem("rms_normed")
        residual = sem("residual")
        gate = [sem(f"gate_{w}") for w in names[:2]]
        pre_act = [sem(f"pre_act_{w}") for w in names[:2]]
        gelu = [sem(f"gelu_{w}") for w in names[:2]]
        w2_done = [sem(f"w2_done_{w}") for w in names[:2]]
        y_copied = [sem(f"y_copied_{w}") for w in names[:2]]
        conv = sem("conv")
        silu_x = sem("silu_x")
        t_part = sem("t_part")
        t_ready = sem("t_ready")
        relu = sem("relu")
        soft = sem("soft")
        dt_ready = sem("dt_ready")
        dtx_ready = sem("dtx_ready")
        decay = sem("decay")
        b_full = sem("b_full")
        c_rows = sem("c_rows")
        c_stored = sem("c_stored")
        order = sem("order")
        c_in = [sem(f"c{k}_in") for k in range(RC)]
        bx = sem("bx")
        scan = sem("scan")
        prod = sem("prod")
        prod_p = sem("prod_p")
        paired = sem("paired")
        added = sem("added")
        summed = sem("summed")
        gated = sem("gated")

        loads = [(Win[:, :], winT), (Wx[:, :, :], wxT[:, 0:R].rearrange("(k p) m -> p k m", p=P)),
                 *[(Wbc[:, :, 2 * N * r:2 * N * (r + 1)], wxT[:, R:R + 2 * N].rearrange("(k p) m -> p k m", p=P))
                   for r in range(3)],
                 (Wdt[:, :], wdtT), (Wo[:, :, :], woT.rearrange("(k p) m -> p k m", p=P)),
                 (Wn[:, :], norm_w), (Wc[:, :, :], conv_w.rearrange("(k p) m -> p k m", p=P)),
                 (Bc[:, :], conv_b), (Bdt[:, :], dt_b),
                 (A[:, :, :], a_log.rearrange("(k p) m -> p k m", p=P)), (D[:, :], d_param),
                 (Wg[:, :], wg), (Bg[:, :], bg),
                 (W1[:, :, :], w1.rearrange("e h i -> h e i")), (W2[:, :, :], w2.rearrange("e i h -> i e h")),
                 *[(b_raw[E * r:E * (r + 1), n, :], b) for r in range(3) for n, b in enumerate((b1, b2))],
                 (Diag[:, :, :], diag), (Block[:, :, :], block), (Id[:, :], ident),
                 (Rank[:, :], rank), (Pick[:, :], pick)]
        N_ZERO = 7
        N_SET = 9

        blk = ctx.enter_context(nc.Block())

        @blk.sync
        def _(sp_):
            for dst, src in loads:
                sp_.dma_start(dst, src).then_inc(weights_in, 16)
            xd = x.rearrange("(t p) h -> p t h", p=P)
            od = out.rearrange("(t p) h -> p t h", p=P)
            sp_.dma_start(X[:, 0:J, :], xd[:, 0:J, :]).then_inc(x_in, 16)
            with sp_.Fori(1, LOOP0 + 3) as c:
                sp_.wait_ge(x_in, 16 * c)
                sp_.dma_start(X[:, bass.ds(J * c, J), :], xd[:, bass.ds(J * c, J), :]).then_inc(x_in, 16)

            def fetch_c(it, n):
                if n == 0:
                    it.wait(sp_, c_stored, 0, 16, 16)
                    sp_.sem_inc(order, 1)
                off, m = (n - RC) // N, (n - RC) % N
                if m in POOL_C:
                    it.wait(sp_, prod_p, off, NP, on_pool(m + 1))
                else:
                    it.wait(sp_, prod, off, NV, m + 1 - on_pool(m + 1))
                sp_.dma_start(cs[:, n % RC, :], c_dram[it.i0 % 2, n:n + 1, :].broadcast_to([P, CH])) \
                    .then_inc(c_in[n % RC], 16)

            def store_x(it):
                dst, src = od[:, bass.ds(it.value(J * (it.i0 - 3), J), J), :], X[:, it.tiles(-3), :]
                it.wait(sp_, x_final, -3, 1, 1)
                sp_.dma_start(dst, src).then_inc(x_out, 16)

            def body(it):
                if it.i0 >= LOOP0 and it.has(3):
                    dst, src = X[:, it.tiles(3), :], xd[:, bass.ds(it.value(J * (it.i0 + 3), J), J), :]
                    it.wait(sp_, x_out, 3 - XR, 16, 16)
                    sp_.sem_inc(order, 1)
                    it.wait(sp_, x_in, 3, 16, 0)
                    sp_.dma_start(dst, src).then_inc(x_in, 16)
                for n in range(N):
                    if n == N - 1 and it.has(1):
                        it.wait(sp_, c_rows, 1, 1, 1)
                        sp_.dma_start(c_dram[(it.i0 + 1) % 2], bcT[N:2 * N, :]).then_inc(c_stored, 16)
                    if it.has(0):
                        fetch_c(it, n)
                    if n == 1 and it.has(-3):
                        store_x(it)
            schedule(sp_, body)
            store_x(Iteration(LAST + 1))
            sp_.wait_ge(x_out, 16 * NCH)
            sp_.wait_ge(c_stored, 16 * NCH)

        @blk.tensor
        def _(pe):
            pe.wait_ge(set_up, N_SET)
            pe.wait_ge(weights_in, 16 * len(loads))

            def transposes(it, name, src):
                b = G_AT[name][0]
                it.wait_free(pe, g_free, name)
                for j in range(J):
                    last = nc.tensor.transpose(G[b][:, P * j:P * (j + 1)], src(j), Id[:, :])
                last.then_inc(g_full[b], 1)

            def product(it, name, rows, terms, wait=True):
                b = G_AT[name][0]
                it.wait_free(pe, g_free, name)
                for k, (lhsT, rhs) in enumerate(terms):
                    last = nc.tensor.matmul(G[b][0:rows, :], lhsT, rhs, start=k == 0, stop=k == len(terms) - 1)
                last.then_inc(g_full[b], 1)

            def first_product(it, w, e):
                off = EXPERT[w]
                if e == 0:
                    it.wait_read(pe, g_free, f"oh_f{w + 1}")
                    if w == 1 and it.has(EXPERT[0]):
                        it.wait(pe, gelu[0], EXPERT[0], E, E)
                else:
                    it.wait(pe, gelu[w], off, E, e)
                nc.tensor.matmul(PH[:, :], Lm[:, e, :], ohT[:, w, :], start=True, stop=False)
                nc.tensor.matmul(PH[:, :], W1[:, e, :], xnT[:, w, :], start=False, stop=True) \
                    .then_inc(pre_act[w], 1)

            def second_product(it, w, e):
                off = EXPERT[w]
                it.wait(pe, gelu[w], off, E, e + 1)
                if e == 0:
                    if w == 0:
                        it.wait(pe, y_copied[1], -3, 1, 1)
                    elif it.i0 + 2 < NCH:
                        it.wait(pe, y_copied[0], 2, 1, 1)
                    else:
                        pe.wait_ge(y_copied[0], NCH)
                    nc.tensor.matmul(PY[:, :], b_part[:, 1, :], ohT[:, w, :], start=True, stop=False)
                nc.tensor.matmul(PY[:, :], W2[:, e, :], hs[:, e % 2, :], start=False, stop=e == E - 1) \
                    .then_inc(w2_done[w], 1)

            def y_transposes(it, w):
                it.wait(pe, y_copied[w], EXPERT[w], 1, 1)
                transposes(it, f"y_f{w + 1}", lambda j: yT[:, P * j:P * (j + 1)])

            def broadcast_b(it, off, n):
                if n == 0:
                    it.wait(pe, t_ready, off, 1, 1)
                it.wait(pe, bx, off, N, n - 1)
                nc.tensor.matmul(PB[n % 2][:, :], Pick[:, n:n + 1].broadcast_to([3 * 2 * N, P]),
                                 T3[:, (it.i0 + off) % 2, :], start=True, stop=True).then_inc(b_full, 1)

            def sum_states(it, off, q):
                if q == 0:
                    it.wait(pe, gated, off, 1, 0)
                    for h in range(HF):
                        nc.tensor.matmul(Y[:, h, :], Dd[:, h, :],
                                         xs[:, (it.i0 + off) % 2, h].rearrange("p b l -> p (b l)"),
                                         start=True, stop=False)
                it.wait(pe, added, off, N // Q, q + 1)
                for h in range(HF):
                    last = nc.tensor.matmul(Y[:, h, :], Id[:, :], pair[:, q % 2, h, :],
                                            start=False, stop=q == N // Q - 1)
                last.then_inc(summed, 1)

            def body(it):
                waiting = []

                def next_unit(units):
                    if units:
                        w, e = units.pop(0)
                        if it.has(EXPERT[w]):
                            first_product(it, w, e)
                            waiting.append((w, e))
                            if len(waiting) > 1:
                                second_product(it, *waiting.pop(0))
                    elif waiting and (not slot_units(s) or waiting[0] == (0, E - 1) and not it.has(EXPERT[1])):
                        second_product(it, *waiting.pop(0))

                for s in range(SLOTS):
                    units = slot_units(s)

                    if s < N - 2 and it.has(0):
                        broadcast_b(it, 0, s + 2)
                    if s >= N - 2 and it.has(1):
                        broadcast_b(it, 1, s + 2 - N)
                    for w in range(2):
                        if s == 0 and it.has(EXPERT[w]):
                            name = f"oh_f{w + 1}"
                            b = G_AT[name][0]
                            it.wait(pe, gate[w], EXPERT[w], 5, 5)
                            it.wait_free(pe, g_free, name)
                            for j in range(J):
                                last = nc.tensor.transpose(Gb[b][0:3 * E, P * j:P * (j + 1)],
                                                           oh[:, w, j].rearrange("p r e -> p (r e)"), Idb[:, :])
                            last.then_inc(g_full[b], 1)
                    c = (it.i0 + 1) % 2
                    xsc = xs[:, c].rearrange("p h b l -> p h (b l)")
                    next_unit(units)
                    if s == 1 and it.has(1):
                        it.before().wait_read(pe, g_free, "ln_p")
                        product(it, "x1", P, [(Win[:, P:2 * P], xrT[:, :])])
                    if s == 3 and it.has(1):
                        product(it, "z0", P, [(Win[:, 2 * P:3 * P], xrT[:, :])])
                    if s == 6 and it.has(1):
                        it.wait(pe, silu_x, 1, 1, 1)
                        product(it, "dtx", P, [(Wx[:, h, :], xsc[:, h, :]) for h in range(HF)])
                    next_unit(units)
                    if s == 2 and it.has(-1):
                        sum_states(it, -1, N // Q - 1)
                    if s % Q == 2 and s > Q and it.has(0):
                        sum_states(it, 0, s // Q - 1)
                    if s == 1 and it.has(1):
                        product(it, "x0", P, [(Win[:, 0:P], xrT[:, :])])
                    if s == 3 and it.has(1):
                        product(it, "z1", P, [(Win[:, 3 * P:4 * P], xrT[:, :])])
                    if s == 6 and it.has(-1):
                        it.wait(pe, gated, -1, 1, 1)
                        it.wait_free(pe, g_free, "out")
                        for j in range(J):
                            for h in range(HF):
                                last = nc.tensor.matmul(G[1][:, P * j:P * (j + 1)], y2[:, h, P * j:P * (j + 1)],
                                                        Wo[:, h, :], start=h == 0, stop=h == HF - 1)
                        last.then_inc(g_full[1], 1)
                    if s == 7 and it.has(2):
                        y_transposes(it, 0)
                    if s == 8 and it.has(1):
                        product(it, "bc", 3 * 2 * N, [(Wbc[:, h, :], xsc[:, h, :]) for h in range(HF)])
                    if s in (9, 10) and it.has(1):
                        h = s - 9
                        it.wait_read(pe, g_free, "dtx")
                        product(it, f"dt{h}", P, [(Wdt[:, P * h:P * (h + 1)], dxs[:, :])])
                    if s == 12 and it.has(-2):
                        y_transposes(it, 1)
                    for w in range(2):
                        if s == (10, 13)[w] and it.has(FRONT[w]):
                            it.wait(pe, normed[w], FRONT[w], 1, 1)
                            transposes(it, f"ln_f{w + 1}", lambda j: xn[:, w, j, :])
                        if s == (12, 14)[w] and it.has(FRONT[w]):
                            name = f"gate_f{w + 1}"
                            b = G_AT[name][0]
                            it.wait_read(pe, g_free, f"ln_f{w + 1}")
                            for j in range(J):
                                last = nc.tensor.matmul(G[b][:, E * j:E * (j + 1)], xnT[:, w, P * j:P * (j + 1)],
                                                        Wg[:, :], start=True, stop=True)
                            last.then_inc(g_full[b], 1)
                    if s == 14 and it.has(2):
                        it.wait(pe, rms_normed, 2, 1, 1)
                        transposes(it, "ln_p", lambda j: xr[:, j, :])

            schedule(pe, body)

        @blk.scalar
        def _(act):
            act.wait_ge(weights_in, 16 * len(loads))
            nc.scalar.activation(A[:, :, :], A[:, :, :], ACT.Exp).then_inc(a_exp, 1)
            act.wait_ge(set_up, N_SET)
            act.wait_ge(zeroed, N_ZERO)

            def copy_out(it, name, dst, rows=P):
                b = G_AT[name][0]
                it.wait_full(act, g_full, name)
                nc.scalar.copy(dst, G[b][0:rows, :]).then_inc(g_free[b], 1)

            def y_copy(it, w):
                off = EXPERT[w]
                it.wait(act, w2_done[w], off, E, E)
                if w == 1 and it.has(2):
                    it.wait_full(act, g_full, "y_f1")
                if w == 0 and it.has(-3):
                    it.before().wait_full(act, g_full, "y_f2")
                if w == 1 and not it.has(2) and it.has(-3):
                    it.before().wait_full(act, g_full, "y_f2")
                if w == 0 and not it.has(-3) and it.has(1):
                    it.before().wait_full(act, g_full, "y_f1")
                nc.scalar.copy(yT[:, :], PY[:, :]).then_inc(y_copied[w], 1)

            def decays(it, off, states):
                for n in states:
                    last = n - 8 if n >= DR else max(m for m in range(N) if DA_AT[m] == n)
                    it.wait(act, scan, 0, N, last + 1)
                    for h in range(HF):
                        nc.scalar.activation(dA[:, DA_AT[n], h, :, 1:L], dt[:, (it.i0 + off) % 2, h, :, 1:L], ACT.Exp,
                                             scale=A[:, h, n:n + 1]).then_inc(decay, 1)

            def body(it):
                c = (it.i0 + 1) % 2
                for s in range(SLOTS):
                    for w, e in slot_units(s):
                        if it.has(EXPERT[w]):
                            if e >= 2:
                                it.wait(act, w2_done[w], EXPERT[w], E, e - 1)
                            it.wait(act, pre_act[w], EXPERT[w], E, e + 1)
                            nc.scalar.activation(hs[:, e % 2, :], PH[:, :], ACT.Gelu).then_inc(gelu[w], 1)
                            if w == 1 and e == 1 and it.has(EXPERT[0]):
                                y_copy(it, 0)
                    if s == 7 and it.has(EXPERT[0]) and not it.has(EXPERT[1]):
                        y_copy(it, 0)
                    if s == 2 and it.has(1):
                        it.wait(act, conv, 1, 2 * (K - 1), 0)
                        for h in (1, 0):
                            it.wait_full(act, g_full, f"x{h}")
                            src = G[h][:, :].rearrange("p (b l) -> p b l", b=NB)
                            nc.scalar.copy(xp[:, h, :, K - 1:K - 1 + L], src)
                            nc.scalar.activation(xs[:, c, h], src, ACT.Identity, scale=Wc[:, h, K - 1:K],
                                                 bias=Bc[:, h:h + 1]).then_inc(g_free[h], 1)
                    if s == 5 and it.has(1):
                        it.wait(act, gated, -1, 1, 1)
                        for h in range(HF):
                            it.wait_full(act, g_full, f"z{h}")
                            nc.scalar.activation(zs[:, c, h, :], G[h][:, :], ACT.Silu).then_inc(g_free[h], 1)
                        it.wait(act, conv, 1, 2 * (K - 1), 2 * (K - 1))
                        nc.scalar.activation(xs[:, c], xs[:, c], ACT.Silu).then_inc(silu_x, 1)
                    if s == 7 and it.has(1):
                        if it.has(-1):
                            it.wait_full(act, g_full, "out")
                        copy_out(it, "dtx", dxs[:, :])
                    if s == 9 and it.has(1):
                        it.wait(act, bx, -1, N, N)
                        it.wait(act, c_stored, 1, 16, 0)
                        it.wait_full(act, g_full, "bc")
                        nc.scalar.copy(bcT[:, :], G[1][0:2 * N, :]).then_inc(c_rows, 1)
                        nc.scalar.copy(T3[:, c, :], G[1][0:3 * 2 * N, :]).then_inc(t_part, 1)
                    if s == 11 and it.has(1):
                        it.wait_read(act, g_free, "bc")
                        nc.scalar.copy(T3[0:2 * 2 * N, c, :], t_rest[0:2 * 2 * N, :]).then_inc(t_part, 1)
                    if s in (9, 10) and it.has(1):
                        h = s - 9
                        if h == 0:
                            it.wait(act, residual, 1, 1, 1)
                        it.wait_full(act, g_full, f"dt{h}")
                        nc.scalar.activation(dt[:, c, h].rearrange("p b l -> p (b l)"), G[0][:, :], ACT.Relu,
                                             bias=Bdt[:, h:h + 1]).then_inc(relu, 1)
                        nc.scalar.activation(sp[:, h, :], G[0][:, :], ACT.Abs, bias=Bdt[:, h:h + 1]) \
                            .then_inc(g_free[0], 1)
                    if s == 11 and it.has(FRONT[0]):
                        copy_out(it, "ln_f1", xnT[:, 0, :])
                    if s == 11 and it.has(EXPERT[1]):
                        y_copy(it, 1)
                    if s == 11 and it.has(0):
                        decays(it, 0, DECAYS[DR:])
                    if s == 12 and it.has(1):
                        it.wait_read(act, g_free, "dt1")
                        nc.scalar.activation(sp[:, :, :], sp[:, :, :], ACT.Exp, scale=-1.0).then_inc(soft, 1)
                        it.wait(act, soft, 1, 2, 1)
                        nc.scalar.activation(sp[:, :, :], sp[:, :, :], ACT.Ln, bias=1.0).then_inc(soft, 1)
                    if s == 13 and it.has(FRONT[1]):
                        copy_out(it, "ln_f2", xnT[:, 1, :])
                    if s == 13 and it.has(1):
                        it.wait(act, dt_ready, 1, 1, 1)
                    if it.has(1) and s >= 13:
                        decays(it, 1, DECAYS[:DR][4 * (s - 13):4 * (s - 12)])
                    if s == 14 and it.has(2):
                        it.wait_full(act, g_full, "ln_p")
                        nc.scalar.copy(xrT[:, :], G[0][:, :]).then_inc(g_free[0], 1)

            schedule(act, body)

        @blk.vector
        def _(dve):
            nc.vector.memset(dA[:, :, :, :, 0:1], 0.0).then_inc(zeroed, 1)
            nc.vector.memset(xp[:, :, :, 0:K - 1], 0.0).then_inc(zeroed, 1)
            nc.vector.memset(half[:, :], -0.5).then_inc(zeroed, 1)
            nc.vector.memset(eps[:, 0], LN_EPS).then_inc(zeroed, 1)
            nc.vector.memset(eps[:, 1], RMS_EPS).then_inc(zeroed, 1)
            nc.vector.memset(ticket[:, 0:1], 0.0).then_inc(zeroed, 1)
            dve.wait_ge(weights_in, 16 * len(loads))
            nc.vector.tensor_copy(Idb[:, :], Id[:, :]).then_inc(zeroed, 1)
            dve.wait_ge(a_exp, 1)
            nc.vector.tensor_scalar(A[:, :, :], A[:, :, :], -1.0, None, ALU.mult).then_inc(set_up, 1)
            nc.vector.tensor_scalar(Win[:, :], Win[:, :], Wn[:, 0:1], None, ALU.mult).then_inc(set_up, 1)
            nc.vector.tensor_copy(b_part[:, :, :], b_raw[:, :, :]).then_inc(set_up, 1)
            for h in range(HF):
                last = nc.vector.tensor_scalar(Dd[:, h, :], Id[:, :], D[:, h:h + 1], None, ALU.mult)
            last.then_inc(set_up, 1)
            dve.wait_ge(set_up, 4)
            nc.vector.tensor_tensor(b_rest[0:2 * E], b_raw[0:2 * E], b_part[0:2 * E], ALU.subtract).then_inc(set_up, 1)
            dve.wait_ge(set_up, 5)
            nc.vector.tensor_copy(b_part[0:2 * E], b_rest[0:2 * E]).then_inc(set_up, 1)
            dve.wait_ge(set_up, 6)
            nc.vector.tensor_tensor(b_part[0:E], b_rest[0:E], b_part[0:E], ALU.subtract).then_inc(set_up, 1)
            dve.wait_ge(set_up, 7)
            nc.vector.tensor_tensor(Diag[:, :, :], Diag[:, :, :],
                                    b_part[:, 0:1, :].broadcast_to([3 * E, E, P]), ALU.mult).then_inc(set_up, 1)
            dve.wait_ge(set_up, 8)
            nc.vector.tensor_tensor(Lm[:, :, :], Diag[:, :, :], Block[:, :, :], ALU.add).then_inc(set_up, 1)
            dve.wait_ge(set_up, N_SET)
            dve.wait_ge(zeroed, N_ZERO)

            def norm_stats(it, w, off):
                if w == 0:
                    dve.wait_ge(set_up, N_SET)
                    it.wait(dve, x_in, off, 16, 16)
                for j in range(J):
                    last = nc.vector.bn_stats(stat[:, w, j, :], X[:, it.tiles(off, j, 1), :])
                last.then_inc(stats[w], 1)
                it.wait(dve, stats[w], off, 1, 1)
                it.wait(dve, scale_ready[w], off, 1, 0)
                nc.vector.tensor_copy(ticket[:, 1:2], ticket[:, 0:1])
                for j in range(J):
                    last = nc.vector.bn_aggr(mv[:, w, j, :], stat[:, w, j, :])
                last.then_inc(moments[w], 1)

            def normalize(it, w, off, dst, scale, done):
                for j in range(J):
                    last = nc.vector.tensor_scalar(dst[:, j:j + 1, :], X[:, it.tiles(off, j, 1), :],
                                                   mv[:, w, j, 0:1], scale[:, j:j + 1], ALU.subtract, ALU.mult)
                last.then_inc(done, 1)

            def state_bx(it, off, n):
                c = (it.i0 + off) % 2
                if n == 0:
                    it.wait(dve, dtx_ready, off, 1, 1)
                it.wait(dve, b_full, off, N, n + 1)
                it.wait(dve, paired, off, N // 2, (n - HR) // 2 + 1)
                nc.vector.tensor_tensor(hb[:, n % HR], dtx[:, c], PB[n % 2][:, None, :].broadcast_to([P, HF, CH]),
                                        ALU.mult).then_inc(bx, 1)

            def state_scan(it, n):
                it.wait(dve, decay, 0, HF * N, HF * (DECAYS.index(n) + 1))
                it.wait(dve, bx, 0, N, n + 1)
                h = hb[:, n % HR].rearrange("p h t -> p (h t)")
                nc.vector.tensor_tensor_scan(h, dA[:, DA_AT[n]].rearrange("p h b l -> p (h b l)"), h, 0.0,
                                             ALU.mult, ALU.add).then_inc(scan, 1)

            def state_prod(it, n):
                if n in POOL_C:
                    return
                it.wait(dve, c_in[n % RC], 0, 16 * (N // RC), 16 * (n // RC + 1))
                it.wait(dve, scan, 0, N, n + 1)
                nc.vector.tensor_tensor(hb[:, n % HR], hb[:, n % HR], cs[:, n % RC, None, :].broadcast_to([P, HF, CH]),
                                        ALU.mult).then_inc(prod, 1)

            def convolve(it, k):
                c = (it.i0 + 1) % 2
                for h in (1, 0):
                    if k == 0:
                        it.wait_read(dve, g_free, f"x{h}")
                    else:
                        it.wait(dve, conv, 1, 2 * (K - 1), 2 * k - h)
                    nc.vector.scalar_tensor_tensor(xs[:, c, h], xp[:, h, :, k:k + L], Wc[:, h, k:k + 1],
                                                   xs[:, c, h], ALU.mult, ALU.add).then_inc(conv, 1)

            def one_hot(it, w):
                off, name = FRONT[w], f"gate_f{w + 1}"
                b = G_AT[name][0]
                it.wait_full(dve, g_full, name)
                nc.vector.tensor_tensor(lg[:, w].rearrange("p j e -> p (j e)"), G[b][:, 0:J * E], Bg[:, :],
                                        ALU.add).then_inc(g_free[b], 1)
                it.wait_read(dve, g_free, name)
                nc.vector.tensor_reduce(mx[:, w, 0], lg[:, w], AX_X, ALU.max).then_inc(gate[w], 1)
                it.wait(dve, gate[w], off, 5, 1)
                nc.vector.tensor_tensor(eq[:, w], lg[:, w], mx[:, w, 0, :, None].broadcast_to([P, J, E]),
                                        ALU.is_ge).then_inc(gate[w], 1)
                it.wait(dve, gate[w], off, 5, 2)
                nc.vector.tensor_tensor(eq[:, w], eq[:, w], Rank[:, :].rearrange("p (j e) -> p j e", j=J),
                                        ALU.mult).then_inc(gate[w], 1)
                it.wait(dve, gate[w], off, 5, 3)
                nc.vector.tensor_reduce(mx[:, w, 1], eq[:, w], AX_X, ALU.max).then_inc(gate[w], 1)
                it.wait(dve, gate[w], off, 5, 4)
                nc.vector.tensor_tensor(oh[:, w], eq[:, w, :, None, :].broadcast_to([P, J, 3, E]),
                                        mx[:, w, 1, :, None, None].broadcast_to([P, J, 3, E]),
                                        ALU.is_equal).then_inc(gate[w], 1)

            def one_hot_out(it, w):
                name = f"oh_f{w + 1}"
                b = G_AT[name][0]
                it.wait_full(dve, g_full, name)
                nc.vector.tensor_copy(ohT[:, w, :], Gb[b][0:3 * E, 0:CH]).then_inc(g_free[b], 1)

            def add_to_x(it, name, off, scale):
                b = G_AT[name][0]
                it.wait_full(dve, g_full, name)
                xc = X[:, it.tiles(off), :]
                nc.vector.scalar_tensor_tensor(xc, G[b][:, :].rearrange("p (j h) -> p j h", j=J), scale, xc,
                                               ALU.mult, ALU.add).then_inc(g_free[b], 1)

            def body(it):
                for s in range(SLOTS):
                    if it.has(0):
                        state_scan(it, s)
                        if s < N - 1:
                            state_bx(it, 0, s + 1)
                        state_prod(it, s)
                    for w in range(2):
                        if s == 0 and it.has(EXPERT[w]):
                            one_hot_out(it, w)
                    if s == 3 and it.has(-1):
                        it.wait(dve, summed, -1, N // Q, N // Q)
                        nc.vector.tensor_tensor(y2[:, :, :], Y[:, :, :], zs[:, (it.i0 - 1) % 2], ALU.mult) \
                            .then_inc(gated, 1)
                    if s in (3, 4) and it.has(1):
                        for k in {3: (0,), 4: (1, 2)}[s]:
                            convolve(it, k)
                    if s == 5 and it.has(3):
                        norm_stats(it, 0, 3)
                    if s == 7 and it.has(3):
                        it.wait(dve, scale_ready[0], 3, 1, 1)
                        normalize(it, 0, 3, xn[:, 0], rstd[:, 0], normed[0])
                    if s == 7 and it.has(-1):
                        it.wait(dve, residual, -1, 1, 1)
                        add_to_x(it, "out", -1, 1.0)
                    if s == 8 and it.has(2):
                        add_to_x(it, "y_f1", 2, 0.5)
                    if s == 9 and it.has(-1):
                        dve.wait_ge(set_up, N_SET)
                        it.wait_read(dve, g_free, "out")
                        norm_stats(it, 1, -1)
                    if s == 10 and it.has(1):
                        c = (it.i0 + 1) % 2
                        it.wait(dve, t_part, 1, 2, 1)
                        nc.vector.tensor_tensor(t_rest[:, :], G[1][0:3 * 2 * N, :], T3[:, c, :],
                                                ALU.subtract).then_inc(g_free[1], 1)
                    if s == 11 and it.has(2):
                        dve.wait_ge(set_up, N_SET)
                        it.wait_read(dve, g_free, "y_f1")
                        norm_stats(it, 2, 2)
                    if s == 11 and it.has(-1):
                        it.wait(dve, scale_ready[1], -1, 1, 1)
                        normalize(it, 1, -1, xn[:, 1], rstd[:, 1], normed[1])
                    if s == 12 and it.has(1):
                        c = (it.i0 + 1) % 2
                        it.wait(dve, t_part, 1, 2, 2)
                        nc.vector.tensor_tensor(T3[0:2 * N, c, :], t_rest[0:2 * N, :], T3[0:2 * N, c, :],
                                                ALU.subtract).then_inc(t_ready, 1)
                    if s == 13 and it.has(-2):
                        add_to_x(it, "y_f2", -2, 0.5)
                    if s == 14 and it.has(-2):
                        it.wait_read(dve, g_free, "y_f2")
                        dve.sem_inc(x_final, 1)
                    if s == 13 and it.has(FRONT[0]):
                        one_hot(it, 0)
                    if s == 13 and it.has(2):
                        it.wait(dve, scale_ready[2], 2, 1, 1)
                        it.wait(dve, dt_ready, 1, 1, 1)
                        normalize(it, 2, 2, xr, rms[:, 1], rms_normed)
                        normalize(it, 2, 2, xn_p, rstd[:, 2], normed[2])
                    if s == N - 1:
                        if it.has(FRONT[1]):
                            one_hot(it, 1)
                        if it.has(1):
                            state_bx(it, 1, 0)

            schedule(dve, body)

        @blk.gpsimd
        def _(pool):
            pool.wait_ge(zeroed, N_ZERO)

            def inverse_root(it, w, off):
                m = 5 if w == 2 else 1
                it.wait(pool, moments[w], off, 1, 1)
                nc.gpsimd.tensor_tensor(vt[:, w, :], mv[:, w, :, 1], eps[:, 0], ALU.add).then_inc(pool_ln[w], 1)
                it.wait(pool, pool_ln[w], off, m, 1)
                it.wait(pool, normed[w], off, 1, 0)
                last = nc.gpsimd.tensor_tensor(rstd[:, w, :], vt[:, w, :], half[:, 0:J], ALU.pow)
                if w < 2:
                    last.then_inc(scale_ready[w], 1)
                    return
                last.then_inc(pool_ln[w], 1)
                it.wait(pool, pool_ln[w], off, m, 2)
                nc.gpsimd.tensor_tensor(vt[:, w, :], rstd[:, w, :], rstd[:, w, :], ALU.mult).then_inc(pool_ln[w], 1)
                it.wait(pool, pool_ln[w], off, m, 3)
                nc.gpsimd.tensor_tensor(vt[:, w, :], vt[:, w, :], mv[:, w, :, 1], ALU.mult).then_inc(pool_ln[w], 1)
                it.wait(pool, pool_ln[w], off, m, 4)
                nc.gpsimd.tensor_tensor(vt[:, w, :], vt[:, w, :], eps[:, 1], ALU.add).then_inc(pool_ln[w], 1)
                it.wait(pool, pool_ln[w], off, m, 5)
                nc.gpsimd.tensor_tensor(rms[:, 0], vt[:, w, :], half[:, 0:J], ALU.pow).then_inc(rms_root, 1)
                it.wait(pool, rms_root, off, 1, 1)
                nc.gpsimd.tensor_tensor(rms[:, 1], rms[:, 0], rstd[:, w, :], ALU.mult).then_inc(scale_ready[w], 1)

            def product_c(it, n):
                it.wait(pool, c_in[n % RC], 0, 16 * (N // RC), 16 * (n // RC + 1))
                it.wait(pool, scan, 0, N, n + 1)
                nc.gpsimd.tensor_tensor(hb[:, n % HR], hb[:, n % HR], cs[:, n % RC, None, :].broadcast_to([P, HF, CH]),
                                        ALU.mult).then_inc(prod_p, 1)

            def add_pair(it, off, q):
                dst = 2 if q % 2 else q // 2 % 2
                it.wait(pool, prod, off, NV, 2 * q + 2 - on_pool(2 * q + 2))
                it.wait(pool, prod_p, off, NP, on_pool(2 * q + 2))
                if q % 2 == 0:
                    it.wait(pool, summed, off, N // Q, q // 2 - 1)
                a = 2 * q % HR
                nc.gpsimd.tensor_tensor(pair[:, dst], hb[:, a], hb[:, a + 1], ALU.add).then_inc(paired, 1)

            def add_four(it, off, q):
                it.wait(pool, paired, off, N // 2, 2 * q + 2)
                nc.gpsimd.tensor_tensor(pair[:, q % 2], pair[:, q % 2], pair[:, 2], ALU.add).then_inc(added, 1)

            def body(it):
                c = (it.i0 + 1) % 2
                for s in range(SLOTS):
                    if s == 0 and it.has(-1):
                        add_pair(it, -1, N // 2 - 1)
                        add_four(it, -1, N // Q - 1)
                    if s == 0 and it.has(1):
                        it.wait(pool, normed[2], 1, 1, 1)
                        xc = X[:, it.tiles(1), :]
                        nc.gpsimd.tensor_tensor(xc, xc, xn_p, ALU.add).then_inc(residual, 1)
                    if s % 2 == 0 and s > 0 and it.has(0):
                        add_pair(it, 0, s // 2 - 1)
                        if s % Q == 0:
                            add_four(it, 0, s // Q - 1)
                    if s in POOL_C and it.has(0):
                        product_c(it, s)
                    if s == 6 and it.has(3):
                        inverse_root(it, 0, 3)
                    if s == 10 and it.has(-1):
                        inverse_root(it, 1, -1)
                    if s == 12 and it.has(2):
                        inverse_root(it, 2, 2)
                    if s == 12 and it.has(1):
                        it.wait(pool, soft, 1, 2, 2)
                        d = dt[:, c].rearrange("p h b l -> p h (b l)")
                        nc.gpsimd.tensor_tensor(d, d, sp[:, :, :], ALU.add).then_inc(dt_ready, 1)
                    if s == 13 and it.has(1):
                        it.wait(pool, dt_ready, 1, 1, 1)
                        it.wait(pool, bx, -1, N, N)
                        nc.gpsimd.tensor_tensor(dtx[:, c], d, xs[:, c].rearrange("p h b l -> p h (b l)"),
                                                ALU.mult).then_inc(dtx_ready, 1)

            rms_root = ctx.enter_context(nc.semaphore("rms_root"))
            schedule(pool, body)



def kernel(**inputs):
    import concourse.bacc as _bacc
    import ml_dtypes as _ml
    from concourse.bass_utils import run_bass_kernel_spmd as _run

    v = {k: np.asarray(a) for k, a in inputs.items()}
    flat = np.ascontiguousarray
    x = v["L0_attn_x"]

    def halves(a):
        return flat(a.reshape(HF, P).T)

    rank = np.tile(np.arange(E, 0, -1, dtype=np.float32), (P, J))
    pick = np.zeros((3, 2 * N, 2 * N), _ml.bfloat16)
    diag = np.zeros((3, E, E, P), np.float32)
    block = np.zeros((3, E, E, P), np.float32)
    for n in range(2 * N):
        pick[:, n, n] = 1.0
    for e in range(E):
        diag[:, e, e, :] = 1.0
        block[2, e, :, :] = -BIG
        block[2, e, e, :] = 0.0
    arrays = {
        "x": flat(x.reshape(NTOK, H)),
        "winT": flat(v["L0_attn_in_proj_w"].T), "wxT": flat(v["L0_attn_x_proj_w"].T),
        "wdtT": flat(v["L0_attn_dt_proj_w"].T), "woT": flat(v["L0_attn_out_proj_w"].T),
        "norm_w": flat(v["L0_attn_norm_w"].reshape(P, 1)),
        "conv_w": flat(v["L0_attn_conv_w"].reshape(DI, K)), "conv_b": halves(v["L0_attn_conv_b"]),
        "dt_b": halves(v["L0_attn_dt_proj_b"]), "a_log": flat(v["L0_attn_A_log"]),
        "d_param": halves(v["L0_attn_D_param"]),
        "wg": flat(v["L0_ffn_Wg"]), "bg": flat(np.tile(v["L0_ffn_bg"], (P, J))),
        "w1": flat(v["L0_ffn_W1"]), "b1": flat(v["L0_ffn_b1"]),
        "w2": flat(v["L0_ffn_W2"]), "b2": flat(v["L0_ffn_b2"]),
        "ident": np.eye(P, dtype=np.float32), "rank": rank,
        "pick": pick.reshape(3 * 2 * N, 2 * N), "diag": diag.reshape(3 * E, E, P),
        "block": block.reshape(3 * E, E, P),
    }
    nc = _bacc.Bacc("TRN2", target_bir_lowering=False, num_devices=1)
    args = [nc.dram_tensor(f"in_{k}", a.shape, mybir.dt.from_np(a.dtype), kind="ExternalInput").ap()
            for k, a in arrays.items()]
    out = nc.dram_tensor("out_0", (NTOK, H), F32, kind="ExternalOutput").ap()
    c_dram = nc.dram_tensor("c_rows", (2, N, CH), F32, kind="Internal").ap()
    macaron_kernel(nc, *args, c_dram, out)
    r = _run(nc, [{f"in_{k}": a for k, a in arrays.items()}], core_ids=[0])
    return r.results[0]["out_0"].reshape(x.shape)
```

```python
from contextlib import ExitStack

import concourse.bass as bass
import numpy as np
from concourse import mybir

F32 = mybir.dt.float32
BF16 = mybir.dt.bfloat16
ALU = mybir.AluOpType
ACT = mybir.ActivationFunctionType
AX_X = mybir.AxisListType.X

P = 128
H = 128
L = 256
NTOK = 32 * L
CH = 2 * L
NB = CH // L
J = CH // P
NCH = NTOK // CH
DI = 256
HF = DI // P
N = 16
SLOTS = N
K = 4
R = 128
E = 8
BIG = 1.0e30
XR = 8
HR = 8
LN_EPS, RMS_EPS = 1e-5, 1e-6

FIRST, LAST = -3, NCH + 1
LOOP0, LOOP1 = 3, NCH - 3

STAGES = [("oh_f1", 2, 1, 0, -1), ("oh_f2", -2, 1, 0, -1), ("x1", 1, 1, 1, 1), ("x0", 1, 0, 0, 1),
          ("z0", 1, 0, 5, 1), ("z1", 1, 1, 3, 0), ("out", -1, 1, 7, 0), ("bc", 1, 0, 8, 0),
          ("dt0", 1, 1, 10, 1), ("dt1", 1, 0, 10, 1), ("ln_f1", 3, 1, 11, 0), ("gate_f1", 3, 1, 11, 1),
          ("ln_f2", -1, 0, 12, 1), ("gate_f2", -1, 0, 13, 1), ("ln_p", 2, 0, 13, 1)]
PE_AT = {name: at for name, _, _, *at in STAGES}
G_SEQ = [(name, bank, off) for name, off, bank, _, _ in sorted(STAGES, key=lambda stage: stage[3:])]
G_AT = {name: (bank, off) for name, bank, off in G_SEQ}
ACT_AT = {"taps": 2.5, "silu": 7.0, "bc": 10.0, "dt0": 10.5, "dt1": 10.5, "ln_f1": 12.0,
          "soft": 12.5, "ln_f2": 12.5, "ln_p": 15.5}
DVE_AT = {"gated": 4.5, "tap0": 5.5, "tap12": 5.5, "stats_f1": 5.5, "norm_f1": 8.0, "out": 8.5,
          "y_f1": 9.0, "stats_f2": 10.5, "stats_p": 11.5, "norm_f2": 11.5, "y_f2": 12.5, "gate_f1": 13.5,
          "norm_p": 14.0, "gate_f2": 15.5}
SUMS, LAST_SUM = (6, 11, 14), 2
POOL_AT = {"residual": 1.0, "root_f1": 6.0, "root_f2": 12.0, "root_p": 12.5, "dt": 12.5, "dtx": 13.5}
UNITS = [0, 1, 1, 2, 2, 2, 1, 2, 2, 1, 1, 1, 0, 0, 0, 0]
assert sum(UNITS) == 2 * E
POOL_C = (0, 1, 4, 6, 7, 10, 14, 15)
DR = 12
DECAYS = [0, 1, 2, 3, 8, 9, 10, 11, 4, 5, 6, 7, 12, 13, 14, 15]
DA_AT = [n if n < DR else n - 8 for n in range(N)]
RB = RC = 4
DECAY_AT = [13, 13, 13, 13, 13, 13, 13, 13, 16, 16, 16, 17, 27, 28, 28, 29]
PAIR_AT = [3, 4, 8, 10, 11, 12, 13, 17]
Q = 4
FOURS = (0, 1, 2, 3)
FRONT = {0: 3, 1: -1}
EXPERT = {0: 2, 1: -2}


def g_uses(i, name):
    bank = G_AT[name][0]
    n = sum(0 <= k + off < NCH for k in range(FIRST, i) for _, b, off in G_SEQ if b == bank)
    for other, b, off in G_SEQ:
        if other == name:
            return n
        n += b == bank and 0 <= i + off < NCH


G_EACH = [sum(b == bank for _, b, _ in G_SEQ) for bank in range(2)]


class Iteration:

    def __init__(self, i0, turn=None):
        self.i0, self.turn = i0, turn

    def value(self, at_i0, each):
        return at_i0 if self.turn is None else at_i0 + 2 * each * self.turn

    def has(self, off):
        return 0 <= self.i0 + off < NCH

    def wait(self, eng, sem, off, each, k):
        n = each * (self.i0 + off) + k
        if n > 0:
            eng.wait_ge(sem, self.value(n, each))

    def wait_full(self, eng, g_full, name):
        bank = G_AT[name][0]
        eng.wait_ge(g_full[bank], self.value(g_uses(self.i0, name) + 1, G_EACH[bank]))

    def wait_read(self, eng, g_free, name):
        bank = G_AT[name][0]
        eng.wait_ge(g_free[bank], self.value(g_uses(self.i0, name) + 1, G_EACH[bank]))

    def wait_free(self, eng, g_free, name):
        bank, n = G_AT[name][0], g_uses(self.i0, name)
        if n > 0:
            eng.wait_ge(g_free[bank], self.value(n, G_EACH[bank]))

    def before(self):
        return Iteration(self.i0 - 1, self.turn)

    def tiles(self, off, j=0, n=J):
        return bass.ds(self.value(J * (self.i0 + off) + j, J) % (J * XR), n)


def schedule(eng, body):
    for i in range(FIRST, LOOP0):
        body(Iteration(i))
    with eng.Fori(0, (LOOP1 - LOOP0) // 2) as turn:
        body(Iteration(LOOP0, turn))
        body(Iteration(LOOP0 + 1, turn))
    for i in range(LOOP0 + (LOOP1 - LOOP0) // 2 * 2, LAST + 1):
        body(Iteration(i))


def on_pool(n):
    return sum(m in POOL_C for m in range(n))


def fours(q):
    return sum(m in FOURS for m in range(q))


NP, NV = on_pool(N), N - on_pool(N)


def slot_units(s):
    at = sum(UNITS[:s])
    return [(u // E, u % E) for u in range(at, at + UNITS[s])]


def macaron_kernel(nc, x, winT, wx, wxT, wdtT, woT, norm_w, conv_w, conv_b, dt_b, a_log, d_param,
                   wg, bg, w1, b1, w2, b2, ident, rank, diag, block, bc_dram, out):
    with ExitStack() as ctx:
        def sb(name, shape, dt=F32):
            return ctx.enter_context(nc.sbuf_tensor(name, shape, dt))

        def psum(name, shape):
            return ctx.enter_context(nc.psum_tensor(name, shape, F32))

        def sem(name):
            return ctx.enter_context(nc.semaphore(name))

        X = sb("X", [P, XR * J, H])
        Win = sb("Win", [P, 2 * DI])
        Wxdt = sb("Wxdt", [P, HF, DI])
        Wbc = sb("Wbc", [P, HF, 2 * N])
        Wo = sb("Wo", [P, HF, H])
        Wn = sb("Wn", [P, 1])
        Wc = sb("Wc", [P, HF, K])
        Bc = sb("Bc", [P, HF])
        Bdt = sb("Bdt", [P, HF])
        A = sb("A", [P, HF, N])
        D = sb("D", [P, HF])
        Dd = sb("Dd", [P, HF, P])
        Wg = sb("Wg", [P, E])
        Bg = sb("Bg", [P, J * E])
        W1 = sb("W1", [P, E, P])
        W2 = sb("W2", [P, E, H])
        b_part = sb("b_part", [3 * E, 2, P], BF16)
        Lm = sb("Lm", [3 * E, E, P], BF16)
        Id = sb("Id", [P, P])
        Idb = sb("Idb", [P, P], BF16)
        Rank = sb("Rank", [P, J * E])
        ticket = sb("ticket", [P, 2])
        eps = sb("eps", [P, 2, J])
        half = sb("half", [P, 2 * J])
        stat = sb("stat", [P, 3, J, 6])
        mv = sb("mv", [P, 3, J, 2])
        vt = sb("vt", [P, 3, J])
        rstd = sb("rstd", [P, 3, J])
        rms = sb("rms", [P, 2, J])
        xn = sb("xn", [P, 2, J, H])
        xnT = sb("xnT", [P, 2, CH])
        lg = sb("lg", [P, 2, J, E])
        eq = sb("eq", [P, 2, J, E])
        mx = sb("mx", [P, 2, 2, J])
        oh = sb("oh", [P, 2, J, 3, E], BF16)
        ohT = sb("ohT", [3 * E, 2, CH], BF16)
        hs = sb("hs", [P, 2, CH])
        xrT = sb("xrT", [P, CH])
        xp = sb("xp", [P, HF, NB, K - 1 + L])
        xs = sb("xs", [P, 2, HF, NB, L])
        zs = sb("zs", [P, 2, HF, CH])
        sp = sb("sp", [P, HF, CH])
        dt = sb("dt", [P, 2, HF, NB, L])
        dtx = sb("dtx", [P, 2, HF, CH])
        dA = sb("dA", [P, DR, HF, NB, L])
        hb = sb("hb", [P, HR, HF, CH])
        pair = sb("pair", [P, 3, HF, CH])
        bs = sb("bs", [P, RB, CH])
        cs = sb("cs", [P, RC, CH])
        bcT = sb("bcT", [2 * N, CH])
        y2 = sb("y2", [P, HF, CH])
        set_buf = [hb[0:3 * E, k].rearrange("p h t -> p (h t)") for k in range(3)]
        Diag = set_buf[0].rearrange("p (e i) -> p e i", e=E)
        Block = set_buf[1].rearrange("p (e i) -> p e i", e=E)
        Wx, Wdt = (hb[:, 3, h, 0:DI] for h in range(HF))
        b_raw = set_buf[2][:, 0:2 * P].rearrange("p (n i) -> p n i", n=2)
        b_rest = set_buf[2][:, 2 * P:4 * P].rearrange("p (n i) -> p n i", n=2)
        xr = y2[:, 0, :].rearrange("p (j h) -> p j h", j=J)
        xn_p = y2[:, 1, :].rearrange("p (j h) -> p j h", j=J)

        G = [psum(f"G{b}", [P, CH]) for b in range(2)]
        PH = [psum(f"PH{k}", [P, CH]) for k in range(2)]
        PY = [psum(f"PY{w}", [P, CH]) for w in range(2)]
        Y = psum("Y", [P, HF, CH])
        Gb = [g[:, :].bitcast(BF16) for g in G]

        first_in = sem("first_in")
        rest_in = sem("rest_in")
        zeroed = sem("zeroed")
        set_up = sem("set_up")
        a_exp = sem("a_exp")
        x_in = sem("x_in")
        x_out = sem("x_out")
        g_full = [sem(f"g{b}_full") for b in range(2)]
        g_free = [sem(f"g{b}_free") for b in range(2)]
        names = ["f1", "f2", "p"]
        stats = [sem(f"stats_{w}") for w in names]
        moments = [sem(f"moments_{w}") for w in names]
        pool_ln = [sem(f"pool_ln_{w}") for w in names]
        scale_ready = [sem(f"scale_{w}") for w in names]
        normed = [sem(f"normed_{w}") for w in names]
        rms_normed = sem("rms_normed")
        residual = sem("residual")
        gate = [sem(f"gate_{w}") for w in names[:2]]
        pre_act = [sem(f"pre_act_{w}") for w in names[:2]]
        gelu = [sem(f"gelu_{w}") for w in names[:2]]
        w2_done = [sem(f"w2_done_{w}") for w in names[:2]]
        y_added = [sem(f"y_added_{w}") for w in names[:2]]
        conv = sem("conv")
        silu_x = sem("silu_x")
        combined = sem("combined")
        relu = sem("relu")
        soft = sem("soft")
        dt_ready = sem("dt_ready")
        dtx_ready = sem("dtx_ready")
        decay = sem("decay")
        bc_stored = sem("bc_stored")
        order = sem("order")
        b_in = [sem(f"b{k}_in") for k in range(RB)]
        c_in = [sem(f"c{k}_in") for k in range(RC)]
        bx = sem("bx")
        scan = sem("scan")
        prod = sem("prod")
        prod_p = sem("prod_p")
        paired = sem("paired")
        added = sem("added")
        summed = sem("summed")
        gated = sem("gated")

        first = [(Id[:, :], ident), (A[:, :, :], a_log.rearrange("(k p) m -> p k m", p=P)), (D[:, :], d_param),
                 *[(b_raw[E * r:E * (r + 1), n, :], b) for r in range(3) for n, b in enumerate((b1, b2))],
                 (Diag[:, :, :], diag), (Block[:, :, :], block), (Wn[:, :], norm_w), (Win[:, :], winT),
                 (Wg[:, :], wg), (Bg[:, :], bg), (Rank[:, :], rank)]
        rest = [(W1[:, :, :], w1.rearrange("e h i -> h e i")), (W2[:, :, :], w2.rearrange("e i h -> i e h")),
                (Wc[:, :, :], conv_w.rearrange("(k p) m -> p k m", p=P)), (Bc[:, :], conv_b),
                (Wx, wx[0:R, :]),
                (Wbc[:, :, :], wxT[:, R:R + 2 * N].rearrange("(k p) m -> p k m", p=P)),
                (Wdt, wdtT), (Bdt[:, :], dt_b), (Wo[:, :, :], woT.rearrange("(k p) m -> p k m", p=P))]
        N_ZERO = 7
        N_SET = 9

        blk = ctx.enter_context(nc.Block())

        @blk.sync
        def _(sp_):
            xd = x.rearrange("(t p) h -> p t h", p=P)
            od = out.rearrange("(t p) h -> p t h", p=P)
            sp_.dma_start(X[:, 0:J, :], xd[:, 0:J, :]).then_inc(x_in, 16)
            for dst, src in first:
                sp_.dma_start(dst, src).then_inc(first_in, 16)
            for dst, src in rest:
                sp_.dma_start(dst, src).then_inc(rest_in, 16)
            with sp_.Fori(1, LOOP0 + 3) as c:
                sp_.wait_ge(x_in, 16 * c)
                sp_.dma_start(X[:, bass.ds(J * c, J), :], xd[:, bass.ds(J * c, J), :]).then_inc(x_in, 16)

            def fetch_b(it, off, n):
                if n == 0:
                    it.wait(sp_, bc_stored, off, 16, 16)
                    sp_.sem_inc(order, 1)
                it.wait(sp_, bx, off, N, n - RB + 1)
                sp_.dma_start(bs[:, n % RB, :], bc_dram[(it.i0 + off) % 2, n:n + 1, :].broadcast_to([P, CH])) \
                    .then_inc(b_in[n % RB], 16)

            def fetch_c(it, n):
                off, m = (n - RC) // N, (n - RC) % N
                if m in POOL_C:
                    it.wait(sp_, prod_p, off, NP, on_pool(m + 1))
                else:
                    it.wait(sp_, prod, off, NV, m + 1 - on_pool(m + 1))
                sp_.dma_start(cs[:, n % RC, :], bc_dram[it.i0 % 2, N + n:N + n + 1, :].broadcast_to([P, CH])) \
                    .then_inc(c_in[n % RC], 16)

            def store_x(it):
                dst, src = od[:, bass.ds(it.value(J * (it.i0 - 3), J), J), :], X[:, it.tiles(-3), :]
                it.wait(sp_, y_added[1], -3, 1, 1)
                sp_.dma_start(dst, src).then_inc(x_out, 16)

            def body(it):
                if it.i0 >= LOOP0 and it.has(3):
                    dst, src = X[:, it.tiles(3), :], xd[:, bass.ds(it.value(J * (it.i0 + 3), J), J), :]
                    it.wait(sp_, x_out, 3 - XR, 16, 16)
                    sp_.sem_inc(order, 1)
                    it.wait(sp_, x_in, 3, 16, 0)
                    sp_.dma_start(dst, src).then_inc(x_in, 16)
                for n in range(N):
                    if it.has(0):
                        fetch_c(it, n)
                        if n < N - 1:
                            fetch_b(it, 0, n + 1)
                    if n == N - 1 and it.has(1):
                        it.wait_read(sp_, g_free, "bc")
                        sp_.dma_start(bc_dram[(it.i0 + 1) % 2], bcT[:, :]).then_inc(bc_stored, 16)
                        fetch_b(it, 1, 0)
                    if n == 1 and it.has(-3):
                        store_x(it)
            schedule(sp_, body)
            store_x(Iteration(LAST + 1))
            sp_.wait_ge(x_out, 16 * NCH)
            sp_.wait_ge(bc_stored, 16 * NCH)

        @blk.tensor
        def _(pe):
            pe.wait_ge(set_up, N_SET)

            def transposes(it, name, src):
                b = G_AT[name][0]
                it.wait_free(pe, g_free, name)
                for j in range(J):
                    last = nc.tensor.transpose(G[b][:, P * j:P * (j + 1)], src(j), Id[:, :])
                last.then_inc(g_full[b], 1)

            def product(it, name, rows, terms, wait=True):
                b = G_AT[name][0]
                it.wait_free(pe, g_free, name)
                for k, (lhsT, rhs) in enumerate(terms):
                    last = nc.tensor.matmul(G[b][0:rows, :], lhsT, rhs, start=k == 0, stop=k == len(terms) - 1)
                last.then_inc(g_full[b], 1)

            def first_product(it, w, e):
                off = EXPERT[w]
                if e == 0:
                    it.wait_read(pe, g_free, f"oh_f{w + 1}")
                if e < 2:
                    if it.has(EXPERT[0]) and w == 1:
                        it.wait(pe, gelu[0], EXPERT[0], E, E)
                    elif it.has(EXPERT[1] - 1) and w == 0:
                        it.wait(pe, gelu[1], EXPERT[1] - 1, E, E)
                    else:
                        it.wait(pe, gelu[w], off, E, 0)
                else:
                    it.wait(pe, gelu[w], off, E, e - 1)
                nc.tensor.matmul(PH[e % 2][:, :], Lm[:, e, :], ohT[:, w, :], start=True, stop=False)
                nc.tensor.matmul(PH[e % 2][:, :], W1[:, e, :], xnT[:, w, :], start=False, stop=True) \
                    .then_inc(pre_act[w], 1)

            def second_product(it, w, e):
                off = EXPERT[w]
                it.wait(pe, gelu[w], off, E, e + 1)
                if e == 0:
                    it.wait(pe, y_added[w], off, 1, 0)
                for j in range(J):
                    if e == 0:
                        nc.tensor.matmul(PY[w][:, P * j:P * (j + 1)], ohT[:, w, P * j:P * (j + 1)], b_part[:, 1, :],
                                         start=j == 0, stop=False)
                    last = nc.tensor.matmul(PY[w][:, P * j:P * (j + 1)], hs[:, e % 2, P * j:P * (j + 1)], W2[:, e, :],
                                            start=False, stop=e == E - 1 and j == J - 1)
                last.then_inc(w2_done[w], 1)

            def sum_states(it, off, q):
                if q == 0:
                    it.wait(pe, gated, off, 1, 0)
                    for h in range(HF):
                        nc.tensor.matmul(Y[:, h, :], Dd[:, h, :],
                                         xs[:, (it.i0 + off) % 2, h].rearrange("p b l -> p (b l)"),
                                         start=True, stop=False)
                if q in FOURS:
                    it.wait(pe, added, off, len(FOURS), fours(q + 1))
                else:
                    it.wait(pe, paired, off, N // 2, 2 * q + 2)
                    for h in range(HF):
                        nc.tensor.matmul(Y[:, h, :], Id[:, :], pair[:, 2, h, :], start=False, stop=False)
                for h in range(HF):
                    last = nc.tensor.matmul(Y[:, h, :], Id[:, :], pair[:, q % 2, h, :],
                                            start=False, stop=q == N // Q - 1)
                last.then_inc(summed, 1)

            def stages(it, c, xsc, s, place):
                def now(name):
                    return PE_AT[name] == [s, place] and it.has(G_AT[name][1])

                if now("x1"):
                    it.before().wait_read(pe, g_free, "ln_p")
                    product(it, "x1", P, [(Win[:, P:2 * P], xrT[:, :])])
                if now("x0"):
                    product(it, "x0", P, [(Win[:, 0:P], xrT[:, :])])
                if now("z0"):
                    product(it, "z0", P, [(Win[:, 2 * P:3 * P], xrT[:, :])])
                if now("z1"):
                    product(it, "z1", P, [(Win[:, 3 * P:4 * P], xrT[:, :])])
                if now("out"):
                    it.wait(pe, gated, -1, 1, 1)
                    it.wait_free(pe, g_free, "out")
                    b = G_AT["out"][0]
                    for j in range(J):
                        for h in range(HF):
                            last = nc.tensor.matmul(G[b][:, P * j:P * (j + 1)], y2[:, h, P * j:P * (j + 1)],
                                                    Wo[:, h, :], start=h == 0, stop=h == HF - 1)
                    last.then_inc(g_full[b], 1)
                if now("bc"):
                    it.wait(pe, silu_x, 1, 1, 1)
                    product(it, "bc", 2 * N, [(Wbc[:, h, :], xsc[:, h, :]) for h in range(HF)])
                for h in range(HF):
                    if now(f"dt{h}"):
                        pe.wait_ge(combined, 2)
                        it.wait(pe, silu_x, 1, 1, 1)
                        product(it, f"dt{h}", P, [(Wxdt[:, k, P * h:P * (h + 1)], xsc[:, k, :]) for k in range(HF)])
                for w in range(2):
                    if now(f"ln_f{w + 1}"):
                        it.wait(pe, normed[w], FRONT[w], 1, 1)
                        transposes(it, f"ln_f{w + 1}", lambda j: xn[:, w, j, :])
                    if now(f"gate_f{w + 1}"):
                        name = f"gate_f{w + 1}"
                        b = G_AT[name][0]
                        it.wait_read(pe, g_free, f"ln_f{w + 1}")
                        it.wait_free(pe, g_free, name)
                        for j in range(J):
                            last = nc.tensor.matmul(G[b][:, E * j:E * (j + 1)], xnT[:, w, P * j:P * (j + 1)],
                                                    Wg[:, :], start=True, stop=True)
                        last.then_inc(g_full[b], 1)
                if now("ln_p"):
                    it.wait(pe, rms_normed, 2, 1, 1)
                    transposes(it, "ln_p", lambda j: xr[:, j, :])

            def body(it):
                if it.i0 == FIRST + 1:
                    pe.wait_ge(rest_in, 16 * len(rest))
                    for k in range(HF):
                        last = nc.tensor.matmul(Y[:, k, 0:DI], Wx[:, P * k:P * (k + 1)], Wdt, start=True, stop=True)
                    last.then_inc(combined, 1)
                waiting = []

                def next_unit(units):
                    if units:
                        w, e = units.pop(0)
                        if it.has(EXPERT[w]):
                            first_product(it, w, e)
                            waiting.append((w, e))
                            if len(waiting) > 1:
                                second_product(it, *waiting.pop(0))
                    elif waiting and (not slot_units(s) or waiting[0] == (0, E - 1) and not it.has(EXPERT[1])):
                        second_product(it, *waiting.pop(0))

                for s in range(SLOTS):
                    units = slot_units(s)

                    for w in range(2):
                        if s == 0 and it.has(EXPERT[w]):
                            name = f"oh_f{w + 1}"
                            b = G_AT[name][0]
                            it.wait(pe, gate[w], EXPERT[w], 5, 5)
                            it.wait_free(pe, g_free, name)
                            for j in range(J):
                                last = nc.tensor.transpose(Gb[b][0:3 * E, P * j:P * (j + 1)],
                                                           oh[:, w, j].rearrange("p r e -> p (r e)"), Idb[:, :])
                            last.then_inc(g_full[b], 1)
                    c = (it.i0 + 1) % 2
                    xsc = xs[:, c].rearrange("p h b l -> p h (b l)")
                    next_unit(units)
                    stages(it, c, xsc, s, 0)
                    next_unit(units)
                    if s == LAST_SUM and it.has(-1):
                        sum_states(it, -1, N // Q - 1)
                    if s in SUMS and it.has(0):
                        sum_states(it, 0, SUMS.index(s))
                    stages(it, c, xsc, s, 1)

            schedule(pe, body)

        @blk.scalar
        def _(act):
            act.wait_ge(first_in, 16 * len(first))
            nc.scalar.activation(A[:, :, :], A[:, :, :], ACT.Exp).then_inc(a_exp, 1)
            act.wait_ge(set_up, N_SET)
            act.wait_ge(zeroed, N_ZERO)

            def copy_out(it, name, dst, rows=P):
                b = G_AT[name][0]
                it.wait_full(act, g_full, name)
                nc.scalar.copy(dst, G[b][0:rows, :]).then_inc(g_free[b], 1)

            def decays(it, off, s):
                for k, n in enumerate(DECAYS):
                    if DECAY_AT[k] != s:
                        continue
                    if k == 0:
                        it.wait(act, dt_ready, off, 1, 1)
                    if n >= DR:
                        it.wait(act, scan, off, N, n - 8 + 1)
                    else:
                        it.wait(act, scan, off - 1, N, max(m for m in range(N) if DA_AT[m] == n) + 1)
                    for h in range(HF):
                        nc.scalar.activation(dA[:, DA_AT[n], h, :, 1:L], dt[:, (it.i0 + off) % 2, h, :, 1:L], ACT.Exp,
                                             scale=A[:, h, n:n + 1]).then_inc(decay, 1)

            def stages(it, t):
                c = (it.i0 + 1) % 2
                if t == ACT_AT["taps"] and it.has(1):
                    it.wait(act, conv, 1, 2 * (K - 1), 0)
                    for h in (1, 0):
                        b = G_AT[f"x{h}"][0]
                        it.wait_full(act, g_full, f"x{h}")
                        src = G[b][:, :].rearrange("p (b l) -> p b l", b=NB)
                        nc.scalar.copy(xp[:, h, :, K - 1:K - 1 + L], src)
                        nc.scalar.activation(xs[:, c, h], src, ACT.Identity, scale=Wc[:, h, K - 1:K],
                                             bias=Bc[:, h:h + 1]).then_inc(g_free[b], 1)
                if t == ACT_AT["silu"] and it.has(1):
                    it.wait(act, gated, -1, 1, 1)
                    for h in range(HF):
                        it.wait_full(act, g_full, f"z{h}")
                        b = G_AT[f"z{h}"][0]
                        nc.scalar.activation(zs[:, c, h, :], G[b][:, :], ACT.Silu).then_inc(g_free[b], 1)
                    it.wait(act, conv, 1, 2 * (K - 1), 2 * (K - 1))
                    nc.scalar.activation(xs[:, c], xs[:, c], ACT.Silu).then_inc(silu_x, 1)
                if t == ACT_AT["bc"] and it.has(1):
                    it.wait(act, bc_stored, 1, 16, 0)
                    copy_out(it, "bc", bcT[:, :], 2 * N)
                for h in range(HF):
                    if t != ACT_AT[f"dt{h}"] or not it.has(1):
                        continue
                    b = G_AT[f"dt{h}"][0]
                    it.wait_full(act, g_full, f"dt{h}")
                    nc.scalar.activation(dt[:, c, h].rearrange("p b l -> p (b l)"), G[b][:, :], ACT.Relu,
                                         bias=Bdt[:, h:h + 1]).then_inc(relu, 1)
                    nc.scalar.activation(sp[:, h, :], G[b][:, :], ACT.Abs, bias=Bdt[:, h:h + 1]) \
                        .then_inc(g_free[b], 1)
                if t == ACT_AT["ln_f1"] and it.has(FRONT[0]):
                    copy_out(it, "ln_f1", xnT[:, 0, :])
                if t == ACT_AT["soft"] and it.has(1):
                    it.wait_read(act, g_free, "dt1")
                    nc.scalar.activation(sp[:, :, :], sp[:, :, :], ACT.Exp, scale=-1.0).then_inc(soft, 1)
                    it.wait(act, soft, 1, 2, 1)
                    nc.scalar.activation(sp[:, :, :], sp[:, :, :], ACT.Ln, bias=1.0).then_inc(soft, 1)
                if t == ACT_AT["ln_f2"] and it.has(FRONT[1]):
                    copy_out(it, "ln_f2", xnT[:, 1, :])
                if t == ACT_AT["ln_p"] and it.has(2):
                    copy_out(it, "ln_p", xrT[:, :])

            def body(it):
                if it.i0 == FIRST + 1:
                    act.wait_ge(combined, 1)
                    nc.scalar.copy(Wxdt[:, :, :], Y[:, :, 0:DI]).then_inc(combined, 1)
                for s in range(SLOTS):
                    stages(it, s)
                    for w, e in slot_units(s):
                        if it.has(EXPERT[w]):
                            if e >= 2:
                                it.wait(act, w2_done[w], EXPERT[w], E, e - 1)
                            it.wait(act, pre_act[w], EXPERT[w], E, e + 1)
                            nc.scalar.activation(hs[:, e % 2, :], PH[e % 2][:, :], ACT.Gelu).then_inc(gelu[w], 1)
                    if it.has(0):
                        decays(it, 0, s + SLOTS)
                    if it.has(1):
                        decays(it, 1, s)
                    stages(it, s + 0.5)

            schedule(act, body)

        @blk.vector
        def _(dve):
            nc.vector.memset(dA[:, :, :, :, 0:1], 0.0).then_inc(zeroed, 1)
            nc.vector.memset(xp[:, :, :, 0:K - 1], 0.0).then_inc(zeroed, 1)
            nc.vector.memset(half[:, :], -0.5).then_inc(zeroed, 1)
            nc.vector.memset(eps[:, 0], LN_EPS).then_inc(zeroed, 1)
            nc.vector.memset(eps[:, 1], RMS_EPS).then_inc(zeroed, 1)
            nc.vector.memset(ticket[:, 0:1], 0.0).then_inc(zeroed, 1)
            dve.wait_ge(first_in, 16 * len(first))
            nc.vector.tensor_copy(Idb[:, :], Id[:, :]).then_inc(zeroed, 1)
            dve.wait_ge(a_exp, 1)
            nc.vector.tensor_scalar(A[:, :, :], A[:, :, :], -1.0, None, ALU.mult).then_inc(set_up, 1)
            nc.vector.tensor_scalar(Win[:, :], Win[:, :], Wn[:, 0:1], None, ALU.mult).then_inc(set_up, 1)
            nc.vector.tensor_copy(b_part[:, :, :], b_raw[:, :, :]).then_inc(set_up, 1)
            for h in range(HF):
                last = nc.vector.tensor_scalar(Dd[:, h, :], Id[:, :], D[:, h:h + 1], None, ALU.mult)
            last.then_inc(set_up, 1)
            dve.wait_ge(set_up, 4)
            nc.vector.tensor_tensor(b_rest[0:2 * E], b_raw[0:2 * E], b_part[0:2 * E], ALU.subtract).then_inc(set_up, 1)
            dve.wait_ge(set_up, 5)
            nc.vector.tensor_copy(b_part[0:2 * E], b_rest[0:2 * E]).then_inc(set_up, 1)
            dve.wait_ge(set_up, 6)
            nc.vector.tensor_tensor(b_part[0:E], b_rest[0:E], b_part[0:E], ALU.subtract).then_inc(set_up, 1)
            dve.wait_ge(set_up, 7)
            nc.vector.tensor_tensor(Diag[:, :, :], Diag[:, :, :],
                                    b_part[:, 0:1, :].broadcast_to([3 * E, E, P]), ALU.mult).then_inc(set_up, 1)
            dve.wait_ge(set_up, 8)
            nc.vector.tensor_tensor(Lm[:, :, :], Diag[:, :, :], Block[:, :, :], ALU.add).then_inc(set_up, 1)
            dve.wait_ge(set_up, N_SET)
            dve.wait_ge(zeroed, N_ZERO)

            def norm_stats(it, w, off):
                if w == 0:
                    dve.wait_ge(set_up, N_SET)
                    it.wait(dve, x_in, off, 16, 16)
                for j in range(J):
                    last = nc.vector.bn_stats(stat[:, w, j, :], X[:, it.tiles(off, j, 1), :])
                last.then_inc(stats[w], 1)
                it.wait(dve, stats[w], off, 1, 1)
                it.wait(dve, scale_ready[w], off, 1, 0)
                nc.vector.tensor_copy(ticket[:, 1:2], ticket[:, 0:1])
                for j in range(J):
                    last = nc.vector.bn_aggr(mv[:, w, j, :], stat[:, w, j, :])
                last.then_inc(moments[w], 1)

            def normalize(it, w, off, dst, scale, done):
                for j in range(J):
                    last = nc.vector.tensor_scalar(dst[:, j:j + 1, :], X[:, it.tiles(off, j, 1), :],
                                                   mv[:, w, j, 0:1], scale[:, j:j + 1], ALU.subtract, ALU.mult)
                last.then_inc(done, 1)

            def state_bx(it, off, n):
                c = (it.i0 + off) % 2
                if n == 0:
                    it.wait(dve, dtx_ready, off, 1, 1)
                it.wait(dve, b_in[n % RB], off, 16 * (N // RB), 16 * (n // RB + 1))
                it.wait(dve, paired, off, N // 2, (n - HR) // 2 + 1)
                nc.vector.tensor_tensor(hb[:, n % HR], dtx[:, c], bs[:, n % RB, None, :].broadcast_to([P, HF, CH]),
                                        ALU.mult).then_inc(bx, 1)

            def state_scan(it, n):
                it.wait(dve, decay, 0, HF * N, HF * (DECAYS.index(n) + 1))
                it.wait(dve, bx, 0, N, n + 1)
                h = hb[:, n % HR].rearrange("p h t -> p (h t)")
                nc.vector.tensor_tensor_scan(h, dA[:, DA_AT[n]].rearrange("p h b l -> p (h b l)"), h, 0.0,
                                             ALU.mult, ALU.add).then_inc(scan, 1)

            def state_prod(it, n):
                if n in POOL_C:
                    return
                it.wait(dve, c_in[n % RC], 0, 16 * (N // RC), 16 * (n // RC + 1))
                it.wait(dve, scan, 0, N, n + 1)
                nc.vector.tensor_tensor(hb[:, n % HR], hb[:, n % HR], cs[:, n % RC, None, :].broadcast_to([P, HF, CH]),
                                        ALU.mult).then_inc(prod, 1)

            def convolve(it, k):
                c = (it.i0 + 1) % 2
                for h in (1, 0):
                    if k == 0:
                        it.wait_read(dve, g_free, f"x{h}")
                    else:
                        it.wait(dve, conv, 1, 2 * (K - 1), 2 * k - h)
                    nc.vector.scalar_tensor_tensor(xs[:, c, h], xp[:, h, :, k:k + L], Wc[:, h, k:k + 1],
                                                   xs[:, c, h], ALU.mult, ALU.add).then_inc(conv, 1)

            def one_hot(it, w):
                off, name = FRONT[w], f"gate_f{w + 1}"
                b = G_AT[name][0]
                it.wait_full(dve, g_full, name)
                nc.vector.tensor_tensor(lg[:, w].rearrange("p j e -> p (j e)"), G[b][:, 0:J * E], Bg[:, :],
                                        ALU.add).then_inc(g_free[b], 1)
                it.wait_read(dve, g_free, name)
                nc.vector.tensor_reduce(mx[:, w, 0], lg[:, w], AX_X, ALU.max).then_inc(gate[w], 1)
                it.wait(dve, gate[w], off, 5, 1)
                nc.vector.tensor_tensor(eq[:, w], lg[:, w], mx[:, w, 0, :, None].broadcast_to([P, J, E]),
                                        ALU.is_ge).then_inc(gate[w], 1)
                it.wait(dve, gate[w], off, 5, 2)
                nc.vector.tensor_tensor(eq[:, w], eq[:, w], Rank[:, :].rearrange("p (j e) -> p j e", j=J),
                                        ALU.mult).then_inc(gate[w], 1)
                it.wait(dve, gate[w], off, 5, 3)
                nc.vector.tensor_reduce(mx[:, w, 1], eq[:, w], AX_X, ALU.max).then_inc(gate[w], 1)
                it.wait(dve, gate[w], off, 5, 4)
                nc.vector.tensor_tensor(oh[:, w], eq[:, w, :, None, :].broadcast_to([P, J, 3, E]),
                                        mx[:, w, 1, :, None, None].broadcast_to([P, J, 3, E]),
                                        ALU.is_equal).then_inc(gate[w], 1)

            def one_hot_out(it, w):
                name = f"oh_f{w + 1}"
                b = G_AT[name][0]
                it.wait_full(dve, g_full, name)
                nc.vector.tensor_copy(ohT[:, w, :], Gb[b][0:3 * E, 0:CH]).then_inc(g_free[b], 1)

            def add_to_x(xc, bank, scale, done):
                nc.vector.scalar_tensor_tensor(xc, bank[:, :].rearrange("p (j h) -> p j h", j=J), scale, xc,
                                               ALU.mult, ALU.add).then_inc(done, 1)

            def add_experts(it, w):
                it.wait(dve, w2_done[w], EXPERT[w], E, E)
                add_to_x(X[:, it.tiles(EXPERT[w]), :], PY[w], 0.5, y_added[w])

            def stages(it, t):
                if t == DVE_AT["gated"] and it.has(-1):
                    it.wait(dve, summed, -1, N // Q, N // Q)
                    if it.has(1):
                        it.wait(dve, residual, 1, 1, 1)
                    nc.vector.tensor_tensor(y2[:, :, :], Y[:, :, :], zs[:, (it.i0 - 1) % 2], ALU.mult) \
                        .then_inc(gated, 1)
                if t == DVE_AT["tap0"] and it.has(1):
                    convolve(it, 0)
                if t == DVE_AT["tap12"] and it.has(1):
                    convolve(it, 1)
                    convolve(it, 2)
                if t == DVE_AT["stats_f1"] and it.has(3):
                    norm_stats(it, 0, 3)
                if t == DVE_AT["norm_f1"] and it.has(3):
                    it.wait(dve, scale_ready[0], 3, 1, 1)
                    normalize(it, 0, 3, xn[:, 0], rstd[:, 0], normed[0])
                if t == DVE_AT["out"] and it.has(-1):
                    it.wait(dve, residual, -1, 1, 1)
                    it.wait_full(dve, g_full, "out")
                    b = G_AT["out"][0]
                    add_to_x(X[:, it.tiles(-1), :], G[b], 1.0, g_free[b])
                if t == DVE_AT["y_f1"] and it.has(2):
                    add_experts(it, 0)
                if t == DVE_AT["stats_f2"] and it.has(-1):
                    dve.wait_ge(set_up, N_SET)
                    it.wait_read(dve, g_free, "out")
                    norm_stats(it, 1, -1)
                if t == DVE_AT["stats_p"] and it.has(2):
                    dve.wait_ge(set_up, N_SET)
                    it.wait(dve, y_added[0], 2, 1, 1)
                    norm_stats(it, 2, 2)
                if t == DVE_AT["norm_f2"] and it.has(-1):
                    it.wait(dve, scale_ready[1], -1, 1, 1)
                    normalize(it, 1, -1, xn[:, 1], rstd[:, 1], normed[1])
                if t == DVE_AT["y_f2"] and it.has(-2):
                    add_experts(it, 1)
                if t == DVE_AT["gate_f1"] and it.has(FRONT[0]):
                    one_hot(it, 0)
                if t == DVE_AT["norm_p"] and it.has(2):
                    it.wait(dve, scale_ready[2], 2, 1, 1)
                    normalize(it, 2, 2, xr, rms[:, 1], rms_normed)
                    normalize(it, 2, 2, xn_p, rstd[:, 2], normed[2])
                if t == DVE_AT["gate_f2"] and it.has(FRONT[1]):
                    one_hot(it, 1)

            def body(it):
                for s in range(SLOTS):
                    stages(it, s)
                    if it.has(0):
                        state_scan(it, s)
                        if s < N - 1:
                            state_bx(it, 0, s + 1)
                        state_prod(it, s)
                    for w in range(2):
                        if s == 0 and it.has(EXPERT[w]):
                            one_hot_out(it, w)
                    stages(it, s + 0.5)
                    if s == N - 1 and it.has(1):
                        state_bx(it, 1, 0)

            schedule(dve, body)

        @blk.gpsimd
        def _(pool):
            pool.wait_ge(zeroed, N_ZERO)

            def inverse_root(it, w, off):
                m = 5 if w == 2 else 1
                it.wait(pool, moments[w], off, 1, 1)
                nc.gpsimd.tensor_tensor(vt[:, w, :], mv[:, w, :, 1], eps[:, 0], ALU.add).then_inc(pool_ln[w], 1)
                it.wait(pool, pool_ln[w], off, m, 1)
                it.wait(pool, normed[w], off, 1, 0)
                last = nc.gpsimd.tensor_tensor(rstd[:, w, :], vt[:, w, :], half[:, 0:J], ALU.pow)
                if w < 2:
                    last.then_inc(scale_ready[w], 1)
                    return
                last.then_inc(pool_ln[w], 1)
                it.wait(pool, pool_ln[w], off, m, 2)
                nc.gpsimd.tensor_tensor(vt[:, w, :], rstd[:, w, :], rstd[:, w, :], ALU.mult).then_inc(pool_ln[w], 1)
                it.wait(pool, pool_ln[w], off, m, 3)
                nc.gpsimd.tensor_tensor(vt[:, w, :], vt[:, w, :], mv[:, w, :, 1], ALU.mult).then_inc(pool_ln[w], 1)
                it.wait(pool, pool_ln[w], off, m, 4)
                nc.gpsimd.tensor_tensor(vt[:, w, :], vt[:, w, :], eps[:, 1], ALU.add).then_inc(pool_ln[w], 1)
                it.wait(pool, pool_ln[w], off, m, 5)
                nc.gpsimd.tensor_tensor(rms[:, 0], vt[:, w, :], half[:, 0:J], ALU.pow).then_inc(rms_root, 1)
                it.wait(pool, rms_root, off, 1, 1)
                nc.gpsimd.tensor_tensor(rms[:, 1], rms[:, 0], rstd[:, w, :], ALU.mult).then_inc(scale_ready[w], 1)

            def product_c(it, n):
                it.wait(pool, c_in[n % RC], 0, 16 * (N // RC), 16 * (n // RC + 1))
                it.wait(pool, scan, 0, N, n + 1)
                nc.gpsimd.tensor_tensor(hb[:, n % HR], hb[:, n % HR], cs[:, n % RC, None, :].broadcast_to([P, HF, CH]),
                                        ALU.mult).then_inc(prod_p, 1)

            def add_pair(it, off, q):
                dst = 2 if q % 2 else q // 2 % 2
                it.wait(pool, prod, off, NV, 2 * q + 2 - on_pool(2 * q + 2))
                it.wait(pool, prod_p, off, NP, on_pool(2 * q + 2))
                if q % 2 == 0:
                    it.wait(pool, summed, off, N // Q, q // 2 - 1)
                else:
                    if (q // 2 - 1) % (N // Q) in FOURS:
                        it.wait(pool, added, off, len(FOURS), fours(q // 2))
                    else:
                        it.wait(pool, summed, off, N // Q, q // 2)
                a = 2 * q % HR
                nc.gpsimd.tensor_tensor(pair[:, dst], hb[:, a], hb[:, a + 1], ALU.add).then_inc(paired, 1)

            def add_four(it, off, q):
                it.wait(pool, paired, off, N // 2, 2 * q + 2)
                nc.gpsimd.tensor_tensor(pair[:, q % 2], pair[:, q % 2], pair[:, 2], ALU.add).then_inc(added, 1)

            def stages(it, t):
                c = (it.i0 + 1) % 2
                d = dt[:, c].rearrange("p h b l -> p h (b l)")
                if t == POOL_AT["residual"] and it.has(1):
                    it.wait(pool, normed[2], 1, 1, 1)
                    xc = X[:, it.tiles(1), :]
                    nc.gpsimd.tensor_tensor(xc, xc, xn_p, ALU.add).then_inc(residual, 1)
                if t == POOL_AT["root_f1"] and it.has(3):
                    inverse_root(it, 0, 3)
                if t == POOL_AT["root_f2"] and it.has(-1):
                    inverse_root(it, 1, -1)
                if t == POOL_AT["root_p"] and it.has(2):
                    inverse_root(it, 2, 2)
                if t == POOL_AT["dt"] and it.has(1):
                    it.wait(pool, soft, 1, 2, 2)
                    nc.gpsimd.tensor_tensor(d, d, sp[:, :, :], ALU.add).then_inc(dt_ready, 1)
                if t == POOL_AT["dtx"] and it.has(1):
                    it.wait(pool, dt_ready, 1, 1, 1)
                    it.wait(pool, bx, -1, N, N)
                    nc.gpsimd.tensor_tensor(dtx[:, c], d, xs[:, c].rearrange("p h b l -> p h (b l)"),
                                            ALU.mult).then_inc(dtx_ready, 1)

            def add_pairs(it, off, s):
                for q in range(N // 2):
                    if PAIR_AT[q] == s:
                        add_pair(it, off, q)
                        if q % 2 == 1 and q // 2 in FOURS:
                            add_four(it, off, q // 2)

            def body(it):
                for s in range(SLOTS):
                    stages(it, s)
                    if it.has(-1):
                        add_pairs(it, -1, s + SLOTS)
                    if it.has(0):
                        add_pairs(it, 0, s)
                    if s in POOL_C and it.has(0):
                        product_c(it, s)
                    stages(it, s + 0.5)

            rms_root = ctx.enter_context(nc.semaphore("rms_root"))
            schedule(pool, body)



def kernel(**inputs):
    import concourse.bacc as _bacc
    from concourse.bass_utils import run_bass_kernel_spmd as _run

    v = {k: np.asarray(a) for k, a in inputs.items()}
    flat = np.ascontiguousarray
    x = v["L0_attn_x"]

    def halves(a):
        return flat(a.reshape(HF, P).T)

    rank = np.tile(np.arange(E, 0, -1, dtype=np.float32), (P, J))
    diag = np.zeros((3, E, E, P), np.float32)
    block = np.zeros((3, E, E, P), np.float32)
    for e in range(E):
        diag[:, e, e, :] = 1.0
        block[2, e, :, :] = -BIG
        block[2, e, e, :] = 0.0
    arrays = {
        "x": flat(x.reshape(NTOK, H)),
        "winT": flat(v["L0_attn_in_proj_w"].T), "wx": flat(v["L0_attn_x_proj_w"]), "wxT": flat(v["L0_attn_x_proj_w"].T),
        "wdtT": flat(v["L0_attn_dt_proj_w"].T), "woT": flat(v["L0_attn_out_proj_w"].T),
        "norm_w": flat(v["L0_attn_norm_w"].reshape(P, 1)),
        "conv_w": flat(v["L0_attn_conv_w"].reshape(DI, K)), "conv_b": halves(v["L0_attn_conv_b"]),
        "dt_b": halves(v["L0_attn_dt_proj_b"]), "a_log": flat(v["L0_attn_A_log"]),
        "d_param": halves(v["L0_attn_D_param"]),
        "wg": flat(v["L0_ffn_Wg"]), "bg": flat(np.tile(v["L0_ffn_bg"], (P, J))),
        "w1": flat(v["L0_ffn_W1"]), "b1": flat(v["L0_ffn_b1"]),
        "w2": flat(v["L0_ffn_W2"]), "b2": flat(v["L0_ffn_b2"]),
        "ident": np.eye(P, dtype=np.float32), "rank": rank,
        "diag": diag.reshape(3 * E, E, P),
        "block": block.reshape(3 * E, E, P),
    }
    nc = _bacc.Bacc("TRN2", target_bir_lowering=False, num_devices=1)
    args = [nc.dram_tensor(f"in_{k}", a.shape, mybir.dt.from_np(a.dtype), kind="ExternalInput").ap()
            for k, a in arrays.items()]
    out = nc.dram_tensor("out_0", (NTOK, H), F32, kind="ExternalOutput").ap()
    bc_dram = nc.dram_tensor("bc_rows", (2, 2 * N, CH), F32, kind="Internal").ap()
    macaron_kernel(nc, *args, bc_dram, out)
    r = _run(nc, [{f"in_{k}": a for k, a in arrays.items()}], core_ids=[0])
    return r.results[0]["out_0"].reshape(x.shape)
```
